# Optimizing a Trainium2 kernel written in Bass

```python
import numpy as np
import jax
import jax.numpy as jnp

def _softmax(x, axis=-1):
    return jax.nn.softmax(x, axis=axis)

def _gelu(x):
    return jax.nn.gelu(x, approximate=True)

def _silu(x):
    return jax.nn.silu(x)

def _sigmoid(x):
    return jax.nn.sigmoid(x)

def _layernorm(x, axis=-1, eps=1e-05):
    m = jnp.mean(x, axis=axis, keepdims=True)
    v = jnp.var(x, axis=axis, keepdims=True)
    return (x - m) / jnp.sqrt(v + eps)

def _scatter_add(tgt, idx, src, axis=0):
    return tgt.at[idx].add(src)

def _segment_sum(src, seg, n):
    return jax.ops.segment_sum(src, seg, n)
kernel_name = 'mk_adj_resnorm_d4_adj_r2_d1d8d0'

def setup_inputs(seed: int=0):
    np.random.seed(seed)
    _w = jnp.asarray

    def _rec_inputs():
        import jax
        import jax.numpy as jnp
        _gk = jax.random.key(seed)
        x = -9.806e-05 + 1 * jax.random.normal(jax.random.fold_in(_gk, 1), (16, 512, 64), jnp.float32)
        _a = jax.random.bernoulli(jax.random.fold_in(_gk, 2), 0.015625, (512, 512))
        _a = jnp.logical_or(_a, jnp.eye(512, dtype=bool))
        _af = _a.astype(jnp.float32)
        _af = _af * jax.random.uniform(jax.random.fold_in(_gk, 3), (512, 512), jnp.float32, 0.05, 1)
        adj = _af
        return (x, adj)
    x, adj = _rec_inputs()

    def _L0_gnn_setup():
        import jax, jax.numpy as jnp
        import numpy as np
        MAX_STEPS = 3
        key = jax.random.key(seed)
        ks = jax.random.split(key, 7)
        B, N, D = (1, 4096, 64)
        return {'causal_vars': jax.random.normal(ks[0], (B, N, D), dtype=jnp.float32), 'adj_matrix': jax.random.uniform(ks[1], (N, N), dtype=jnp.float32), 'intervention_value': jax.random.normal(ks[2], (B, D), dtype=jnp.float32), 'W1': jax.random.normal(ks[3], (D, 2 * D), dtype=jnp.float32) * (1.0 / np.sqrt(2 * D)), 'b1': jax.random.normal(ks[4], (D,), dtype=jnp.float32) * 0.01, 'W2': jax.random.normal(ks[5], (D, D), dtype=jnp.float32) * (1.0 / np.sqrt(D)), 'b2': jax.random.normal(ks[6], (D,), dtype=jnp.float32) * 0.01, 'intervention_idx': 0}
    _L0_gnn_all = _L0_gnn_setup()
    _L0_gnn_in = {k: v for k, v in _L0_gnn_all.items() if k in ('intervention_value', 'W1', 'b1', 'W2', 'b2')}
    del _L0_gnn_all

    def _L1_gnn_setup():
        import jax, jax.numpy as jnp
        import numpy as np
        NEG_INF = -1e+16

        def gat_layer(x, graph, W, b):
            h = x @ W
            s = jnp.einsum('bnd,bmd->bnm', h, h) * graph
            s = jnp.where(s == 0.0, NEG_INF, s)
            a = jax.nn.softmax(s, axis=2)
            return jnp.einsum('bnm,bmd->bnd', a, h) + b
        key = jax.random.key(seed)
        k1, k2, k3, k4, k5, k6 = jax.random.split(key, 6)
        B, N, C_IN, HID, HEADS, C_OUT = (16, 512, 64, 128, 8, 64)
        flow_x = jax.random.normal(k1, (B, N, C_IN), dtype=jnp.float32)
        graph = jax.random.randint(k2, (N, N), 0, 2).astype(jnp.float32)
        Wh = jax.random.normal(k3, (HEADS, C_IN, HID), dtype=jnp.float32)
        bh = jax.random.normal(k4, (HEADS, HID), dtype=jnp.float32)
        W_out = jax.random.normal(k5, (HID * HEADS, C_OUT), dtype=jnp.float32)
        b_out = jax.random.normal(k6, (C_OUT,), dtype=jnp.float32)
        return {'flow_x': flow_x, 'graph': graph, 'Wh': Wh, 'bh': bh, 'W_out': W_out, 'b_out': b_out}
    _L1_gnn_all = _L1_gnn_setup()
    _L1_gnn_in = {k: v for k, v in _L1_gnn_all.items() if k in ('Wh', 'bh', 'W_out', 'b_out')}
    del _L1_gnn_all

    def _L2_gnn_setup():
        import jax, jax.numpy as jnp
        import numpy as np
        key = jax.random.key(seed)
        k1, k2, k3 = jax.random.split(key, 3)
        B, N, D = (4, 4096, 64)
        X = jax.random.normal(k1, (B, N, D), dtype=jnp.float32)
        A = jax.random.uniform(k2, (N, N), dtype=jnp.float32)
        W = jax.random.truncated_normal(k3, -2.0, 2.0, (D, D), dtype=jnp.float32) * 0.05
        return {'X': X, 'A': A, 'W': W}
    _L2_gnn_all = _L2_gnn_setup()
    _L2_gnn_in = {k: v for k, v in _L2_gnn_all.items() if k in ('W',)}
    del _L2_gnn_all

    def _L3_gnn_setup():
        import jax, jax.numpy as jnp
        import numpy as np
        ALPHA = 0.2
        key = jax.random.key(seed)
        k1, k2, k3, k4 = jax.random.split(key, 4)
        B, N, Din, Dout = (8, 1024, 64, 64)
        x = jax.random.normal(k1, (B, N, Din), dtype=jnp.float32)
        adj = (jax.random.uniform(k2, (N, N)) < 0.05).astype(jnp.float32)
        lim_w = float(np.sqrt(6.0 / (Din + Dout)))
        weight = jax.random.uniform(k3, (Din, Dout), dtype=jnp.float32, minval=-lim_w, maxval=lim_w)
        lim_a = float(np.sqrt(6.0 / (2 * Dout + 1)))
        a = jax.random.uniform(k4, (2 * Dout, 1), dtype=jnp.float32, minval=-lim_a, maxval=lim_a)
        bias = jnp.zeros((Dout,), dtype=jnp.float32)
        return {'x': x, 'adj': adj, 'weight': weight, 'a': a, 'bias': bias}
    _L3_gnn_all = _L3_gnn_setup()
    _L3_gnn_in = {k: v for k, v in _L3_gnn_all.items() if k in ('weight', 'a', 'bias')}
    del _L3_gnn_all
    return {'x': x, 'adj': adj, 'L0_gnn_intervention_value': _L0_gnn_in['intervention_value'], 'L0_gnn_W1': _L0_gnn_in['W1'], 'L0_gnn_b1': _L0_gnn_in['b1'], 'L0_gnn_W2': _L0_gnn_in['W2'], 'L0_gnn_b2': _L0_gnn_in['b2'], 'L1_gnn_Wh': _L1_gnn_in['Wh'], 'L1_gnn_bh': _L1_gnn_in['bh'], 'L1_gnn_W_out': _L1_gnn_in['W_out'], 'L1_gnn_b_out': _L1_gnn_in['b_out'], 'L2_gnn_W': _L2_gnn_in['W'], 'L3_gnn_weight': _L3_gnn_in['weight'], 'L3_gnn_a': _L3_gnn_in['a'], 'L3_gnn_bias': _L3_gnn_in['bias']}

def reference(x, adj, L0_gnn_intervention_value, L0_gnn_W1, L0_gnn_b1, L0_gnn_W2, L0_gnn_b2, L1_gnn_Wh, L1_gnn_bh, L1_gnn_W_out, L1_gnn_b_out, L2_gnn_W, L3_gnn_weight, L3_gnn_a, L3_gnn_bias):
    import jax
    import jax.numpy as jnp

    def _L0_gnn_ref(causal_vars, adj_matrix, intervention_value, W1, b1, W2, b2, intervention_idx):
        import jax, jax.numpy as jnp
        import numpy as np
        MAX_STEPS = 3
        v = causal_vars.at[:, intervention_idx].set(intervention_value)
        for _ in range(MAX_STEPS):
            effects = jnp.einsum('nm,bmd->bnd', adj_matrix, v)
            h = jnp.concatenate([v, effects], axis=-1)
            h = jax.nn.relu(jnp.einsum('bnk,dk->bnd', h, W1) + b1)
            v = jnp.einsum('bnk,dk->bnd', h, W2) + b2
        return v

    def _L1_gnn_ref(flow_x, graph, Wh, bh, W_out, b_out):
        import jax, jax.numpy as jnp
        import numpy as np
        NEG_INF = -1e+16

        def gat_layer(x, graph, W, b):
            h = x @ W
            s = jnp.einsum('bnd,bmd->bnm', h, h) * graph
            s = jnp.where(s == 0.0, NEG_INF, s)
            a = jax.nn.softmax(s, axis=2)
            return jnp.einsum('bnm,bmd->bnd', a, h) + b
        heads = jax.vmap(lambda W, b: gat_layer(flow_x, graph, W, b))(Wh, bh)
        H, B, N, D = heads.shape
        cat = jnp.moveaxis(heads, 0, 2).reshape(B, N, H * D)
        x = jax.nn.leaky_relu(cat, negative_slope=0.01)
        out = gat_layer(x, graph, W_out, b_out)
        return jax.nn.leaky_relu(out, negative_slope=0.01)

    def _L2_gnn_ref(X, A, W):
        import jax, jax.numpy as jnp
        import numpy as np
        n = A.shape[0]
        A_td = A + jnp.eye(n, dtype=A.dtype)
        deg = jnp.sum(A_td, axis=1)
        dinv = jax.lax.rsqrt(deg)
        A_hat = dinv[:, None] * A_td * dinv[None, :]
        H = jnp.einsum('bmd,nm->bnd', X, A_hat)
        X_p = jnp.einsum('bnd,kd->bnk', H, W)
        return X_p

    def _L3_gnn_ref(x, adj, weight, a, bias):
        import jax, jax.numpy as jnp
        import numpy as np
        ALPHA = 0.2
        N = adj.shape[0]
        adj = adj.at[jnp.diag_indices(N)].set(1.0)
        h = jnp.einsum('bni,io->bno', x, weight)
        D = h.shape[-1]
        e_src = h @ a[:D, 0]
        e_dst = h @ a[D:, 0]
        e = jax.nn.leaky_relu(e_src[:, :, None] + e_dst[:, None, :], negative_slope=ALPHA)
        e = adj[None, :, :] * e
        attention = jax.nn.softmax(e, axis=-1)
        h_prime = jnp.einsum('bij,bjd->bid', attention, h)
        return h_prime + bias
    x = _layernorm(x + _L0_gnn_ref(x, adj, L0_gnn_intervention_value, L0_gnn_W1, L0_gnn_b1, L0_gnn_W2, L0_gnn_b2, 0), axis=-1)
    x = _layernorm(x + _L1_gnn_ref(x, adj, L1_gnn_Wh, L1_gnn_bh, L1_gnn_W_out, L1_gnn_b_out), axis=-1)
    x = _layernorm(x + _L2_gnn_ref(x, adj, L2_gnn_W), axis=-1)
    x = _layernorm(x + _L3_gnn_ref(x, adj, L3_gnn_weight, L3_gnn_a, L3_gnn_bias), axis=-1)
    return x

_drawn_inputs = setup_inputs


def setup_inputs(seed=0):
    import zlib

    import numpy as np

    out = dict(_drawn_inputs(seed))
    spreads = {'L3_gnn_bias': (0.0, 0.1)}
    factors = {'L0_gnn_intervention_value': 5.617,
     'L0_gnn_b1': 5.249,
     'L1_gnn_b_out': 7.919,
     'L3_gnn_a': 8.0}
    for name, (base, spread) in spreads.items():
        noise = np.random.default_rng([zlib.crc32(name.encode()), seed]).standard_normal(out[name].shape)
        drawn = base * np.exp(spread * noise) if base else spread * noise
        out[name] = jnp.asarray(drawn.astype(out[name].dtype))
    for name, factor in factors.items():
        out[name] = (out[name] * factor).astype(out[name].dtype)
    return out
```

```python
from contextlib import ExitStack

import concourse.bass as bass
from concourse import mybir

ALU = mybir.AluOpType
ACT = mybir.ActivationFunctionType
AX = mybir.AxisListType
F32 = mybir.dt.float32
F32R = mybir.dt.float32r
I32 = mybir.dt.int32

P = 128
B = 16
N = 512
D = 64
T = N // P
HEADS = 8
HID = 128
LN_EPS = 1e-5
LOWEST = -3.0e38


def value_wait(engine, semaphore, value):
    if not (isinstance(value, int) and value <= 0):
        engine.wait_ge(semaphore, value)


def exists(index, total):
    return 0 <= index < total if isinstance(index, int) else True


def gnn_stack_program(nc, x, adj, iv, W1, b1, W2, b2, Wh, bh, Wo, bo, W_l2, W_l3, a_l3, bias_l3, out):
    with ExitStack() as ctx:
        def sb(name, shape, dt=F32):
            return ctx.enter_context(nc.sbuf_tensor(name, shape, dt))

        def sem(name):
            return ctx.enter_context(nc.semaphore(name))

        X = sb("X", [P, T, B * D])
        G = sb("G", [P, B * T * D])
        V = G[:, :].rearrange("p (t c) -> p t c", t=T)
        XT = sb("XT", [D, B * N])
        A = sb("A", [P, T, N])
        AT = sb("AT", [P, T, N])
        A1 = sb("A1", [P, T, N])
        ident = sb("ident", [P, P])
        zeros = sb("zeros", [P, 1])
        w_dup = sb("w_dup", [D, 4, 2, D])
        w_bd = sb("w_bd", [P, 4, P])
        b1_col = sb("b1_col", [P, 1])
        b2_col = sb("b2_col", [P, 1])
        wh_slot = [sb(f"wh_slot{s}", [D, HID]) for s in range(2)]
        bb_slot = [sb(f"bb_slot{s}", [P, HID]) for s in range(2)]
        wo_slot = [sb(f"wo_slot{s}", [P, D]) for s in range(2)]
        bo_bc = sb("bo_bc", [P, D])
        W3_sb = sb("W3_sb", [D, 2, D])
        id_src = sb("id_src", [D, D + 2])
        a_dst = sb("a_dst", [D, 1])
        a_dst_bc = sb("a_dst_bc", [D, P])
        bias3_bc = sb("bias3_bc", [P, D])
        v_st = [sb(f"v_st{s}", [P, T, 2 * D]) for s in range(2)]
        vT_sb = [sb(f"vT_sb{s}", [P, N]) for s in range(2)]
        eT_sb = [sb(f"eT_sb{s}", [P, N]) for s in range(2)]
        hT_sb = [sb(f"hT_sb{s}", [P, N]) for s in range(2)]
        GR = T * B
        mean = sb("mean", [P, GR])
        vare = sb("vare", [P, GR])
        root = sb("root", [P, GR])
        rstd = sb("rstd", [P, GR])
        newt = sb("newt", [P, GR])
        newt2 = sb("newt2", [P, GR])
        deg = sb("deg", [P, T])
        dinv = sb("dinv", [P, T])
        x_st = [sb(f"x_st{s}", [P, T, D]) for s in range(4)]
        hf = sb("hf", [P, 2, N])
        hr = sb("hr", [P, 2, N], F32R)
        hl = sb("hl", [P, 2, N], F32R)
        hb = sb("hb", [P, 2, T, HID])
        sc = sb("sc", [P, 4, N])
        ex = sb("ex", [P, 4, N])
        pr = sb("pr", [P, 4, N])
        pT = sb("pT", [P, 2, T, N])
        t1 = sb("t1", [P, 2, N])
        lr = sb("lr", [P, 2, N])
        rel = sb("rel", [P, N])
        z = sb("z", [P, N])
        mx = sb("mx", [P, 4])
        ng = sb("ng", [P, 4])
        cc = sb("cc", [P, 4])
        ls = sb("ls", [P, 2, T])
        rc = sb("rc", [P, 2, T])
        y = sb("y", [P, T, D])
        y2 = sb("y2", [P, T, D])

        banks = [ctx.enter_context(nc.psum_tensor(f"bank{i}", [P, N], F32)) for i in range(8)]

        s_x = sem("s_x")
        s_v = sem("s_v")
        s_iv = sem("s_iv")
        s_adj = sem("s_adj")
        s_wts = sem("s_wts")
        s_ones = sem("s_ones")
        s_wdup_pe = sem("s_wdup_pe")
        s_bd0 = sem("s_bd0")
        s_bd = sem("s_bd")
        s_idp = sem("s_idp")
        s_id = sem("s_id")
        s_a1 = sem("s_a1")
        s_at_pe = sem("s_at_pe")
        s_at = sem("s_at")
        s_adb = sem("s_adb")
        s_l0_stage = [sem(f"s_l0_stage{s}") for s in range(2)]
        s_l0_pe = [sem(f"s_l0_pe{s}") for s in range(2)]
        s_l0_ev = [sem(f"s_l0_ev{s}") for s in range(2)]
        s_deg = sem("s_deg")
        s_l2_stage = [sem(f"s_l2_stage{s}") for s in range(2)]
        s_l2_pe = [sem(f"s_l2_pe{s}") for s in range(2)]
        s_l2_ev = [sem(f"s_l2_ev{s}") for s in range(2)]
        s_ln = [sem(f"s_ln{j}") for j in range(4)]
        s_xt_st = [sem(f"s_xt_st{j}") for j in range(2)]
        s_xt_pe = [sem(f"s_xt_pe{j}") for j in range(2)]
        s_xt = [sem(f"s_xt{j}") for j in range(2)]
        s_out = sem("s_out")

        s_wh = [sem(f"s_wh{s}") for s in range(2)]
        s_bb = [sem(f"s_bb{s}") for s in range(2)]
        s_wo = [sem(f"s_wo{s}") for s in range(2)]
        s_gz = sem("s_gz")
        s_deg2 = sem("s_deg2")

        N_WTS = 8 + 4 + 7
        LN_CENTERED, LN_VAR, LN_STEPS, DEG_STEPS = 3, 6, 13, 7
        STEPS = 3
        GROUPS0 = 1 + 4 * STEPS

        class AttentionPhase:

            def __init__(self, kind, units, k):
                self.kind, self.units, self.tiles, self.k = kind, units, units * T, k
                self.stage = sem(f"{kind}_stage")
                self.h_pe = sem(f"{kind}_h_pe")
                self.hf = sem(f"{kind}_hf")
                self.hr = sem(f"{kind}_hr")
                self.hl = sem(f"{kind}_hl")
                self.hn_pe = sem(f"{kind}_hn_pe")
                self.hb = sem(f"{kind}_hb")
                self.S = sem(f"{kind}_S")
                self.t1 = sem(f"{kind}_t1")
                self.lr = sem(f"{kind}_lr")
                self.mx = sem(f"{kind}_mx")
                self.neg = sem(f"{kind}_neg")
                self.E = sem(f"{kind}_E")
                self.P = sem(f"{kind}_P")
                self.T = sem(f"{kind}_T")
                self.PT = sem(f"{kind}_PT")
                self.rec = sem(f"{kind}_rec")
                self.AV = sem(f"{kind}_AV")
                self.rel = sem(f"{kind}_rel")
                self.y = sem(f"{kind}_y")
                self.z = sem(f"{kind}_z")
                self.G_pe = sem(f"{kind}_G_pe")
                self.G = sem(f"{kind}_G")

        heads = AttentionPhase("heads", B * HEADS, HID)
        outer = AttentionPhase("outer", B, D)
        last = AttentionPhase("last", B, D)

        def iterations(engine, units, body):
            pairs = units // 2
            for i in (-1, 0, 1):
                body(i)
            with engine.Fori(2, pairs - 1) as i:
                body(i)
            for i in (pairs - 1, pairs):
                body(i)

        def batch_of(ph, i, unit_in_pair):
            carry, u = divmod(unit_in_pair, 2)
            return (i + carry) % B if ph.kind == "heads" else 2 * (i + carry) + u

        block = ctx.enter_context(nc.Block())

        @block.sync
        def _(sp):
            for t in range(T):
                sp.dma_start(A[:, t, :], adj[t * P:(t + 1) * P, :]).then_inc(s_adj, 16)
            for t in range(T):
                sp.dma_start(V[:, t, :].rearrange("p (b d) -> p b d", b=B),
                             x[:, t * P:(t + 1) * P, :].rearrange("b p d -> p b d")).then_inc(s_v, 16)
            sp.wait_ge(s_v, 16 * T)
            for b in range(B):
                sp.dma_start(V[0:1, 0, b * D:(b + 1) * D], iv).then_inc(s_iv, 16)
            for t in range(T):
                sp.dma_start(X[:, t, :].rearrange("p (b d) -> p b d", b=B),
                             x[:, t * P:(t + 1) * P, :].rearrange("b p d -> p b d")).then_inc(s_x, 16)

            def head_weights(i):
                for u in range(2):
                    if exists(i, B * HEADS // 2):
                        value_wait(sp, heads.h_pe, 2 * i + u - 1)
                        sp.dma_start(wh_slot[u][:, :], Wh[bass.ds(i // B * 2 + u, 1), :, :]
                                     .rearrange("a i o -> (a i) o")).then_inc(s_wh[u], 16)
                        value_wait(sp, heads.hb, 2 * i + u - 1)
                        sp.dma_start(bb_slot[u][:, :], bh[bass.ds(i // B * 2 + u, 1), :].to_broadcast([P, HID]))\
                          .then_inc(s_bb[u], 16)
                    if exists(i - 1, B * HEADS // 2):
                        value_wait(sp, heads.G_pe, 2 * (i - 1) + u - 1)
                        sp.dma_start(wo_slot[u][:, :], Wo[bass.ds(((i - 1) // B * 2 + u) * HID, HID), :])\
                          .then_inc(s_wo[u], 16)
            for i in (0, 1):
                head_weights(i)
            with sp.Fori(2, B * HEADS // 2) as i:
                head_weights(i)
            head_weights(B * HEADS // 2)

            sp.wait_ge(s_ln[3], LN_STEPS)
            for t in range(T):
                sp.dma_start(out[:, t * P:(t + 1) * P, :].rearrange("b p d -> p b d"),
                             X[:, t, :].rearrange("p (b d) -> p b d", b=B)).then_inc(s_out, 16)
            sp.wait_ge(s_out, 16 * T)

        @block.gpsimd
        def _(pool):
            def after_wait():
                pool.nop(nofuse=True)

            nc.gpsimd.memset(ident[:, :], 0.0).then_inc(s_idp, 1)
            nc.gpsimd.memset(w_bd[:, :, :], 0.0).then_inc(s_bd0, 1)
            pool.wait_ge(s_idp, 1)
            nc.gpsimd.affine_select(out=ident[:, :], in_=ident[:, :], compare_op=ALU.not_equal, fill=1.0,
                                    base=0, pattern=[[-1, P]], channel_multiplier=1).then_inc(s_id, 1)
            pool.wait_ge(s_adj, 16 * T)
            for t in range(T):
                nc.gpsimd.affine_select(out=A1[:, t, :], in_=A[:, t, :], compare_op=ALU.not_equal, fill=1.0,
                                        base=t * P, pattern=[[-1, N]], channel_multiplier=1).then_inc(s_a1, 1)

            def stage0(i):
                for s in range(2):
                    if i == 0 if isinstance(i, int) else False:
                        pool.wait_ge(s_iv, 16 * B)
                    else:
                        pool.wait_ge(s_l0_ev[s], GROUPS0 * i)
                    after_wait()
                    pool.tensor_copy(v_st[s][:, :, :],
                                     V[:, :, bass.ds((2 * i + s) * 2 * D, 2 * D)]).then_inc(s_l0_stage[s], 1)

            stage0(0)
            with pool.Fori(1, B // 4) as i:
                stage0(i)

            def attention(ph):
                def body(i):
                    for k in range(8):
                        u, t = k // T, k % T
                        q, n = 2 * i + u, 8 * i + k
                        if exists(n, ph.tiles):
                            value_wait(pool, ph.mx, n + 1)
                            value_wait(pool, ph.E if ph.kind == "last" else ph.P, n - 3)
                            after_wait()
                            if ph.kind != "last":
                                pool.tensor_scalar(cc[:, n_slot(k):n_slot(k) + 1], mx[:, n_slot(k):n_slot(k) + 1],
                                                   0.0, None, ALU.is_equal)
                            pool.tensor_scalar(ng[:, n_slot(k):n_slot(k) + 1], mx[:, n_slot(k):n_slot(k) + 1],
                                               -1.0, None, ALU.mult).then_inc(ph.neg, 1)
                        if t == 1 and ph.kind != "last" and exists(q + 1, ph.units):
                            w = (u + 1) % 2
                            value_wait(pool, ph.hr, q + 2)
                            after_wait()
                            pool.tensor_tensor(hl[0:ph.k, w, :], hf[0:ph.k, w, :], hr[0:ph.k, w, :].bitcast(F32),
                                               ALU.subtract).then_inc(ph.hl, 1)
                        if t == 3 and ph.kind == "outer" and exists(q + 2, ph.units):
                            value_wait(pool, ph.h_pe, q + 2)
                            after_wait()
                            pool.tensor_copy(x_st[0][:, :, :], G[:, bass.ds(batch_of(ph, i, u + 2) * T * D, T * D)]
                                             .rearrange("p (t d) -> p t d", t=T)).then_inc(ph.stage, 1)
                if ph.kind == "outer":
                    pool.wait_ge(heads.G, heads.units)
                iterations(pool, ph.units, body)

            def n_slot(k):
                return k % 4

            def stage_xt(j):
                pool.wait_ge(s_ln[2 * j], LN_STEPS)

                def body(i):
                    for s in range(4):
                        value_wait(pool, s_xt_pe[j], 4 * i)
                        after_wait()
                        pool.tensor_copy(x_st[s][:, :, :],
                                         X[:, :, bass.ds((4 * i + s) * D, D)]).then_inc(s_xt_st[j], 1)
                body(0)
                with pool.Fori(1, B // 4) as i:
                    body(i)

            stage_xt(0)
            attention(heads)
            attention(outer)
            stage_xt(1)
            attention(last)

        @block.scalar
        def _(act):
            for j, w in enumerate((W1[:, 0:D], W1[:, D:2 * D], W2, W_l2)):
                for c in range(2):
                    act.dma_start(w_dup[:, j, c, :], w).then_inc(s_wts, 16)
            for c in range(2):
                act.dma_start(b1_col[c * D:(c + 1) * D, :], b1.rearrange("(p a) -> p a", a=1)).then_inc(s_wts, 16)
                act.dma_start(b2_col[c * D:(c + 1) * D, :], b2.rearrange("(p a) -> p a", a=1)).then_inc(s_wts, 16)
            act.dma_start(bo_bc[:, :], bo.partition_broadcast(P)).then_inc(s_wts, 16)
            act.dma_start(bias3_bc[:, :], bias_l3.partition_broadcast(P)).then_inc(s_wts, 16)
            for c in range(2):
                act.dma_start(W3_sb[:, c, :], W_l3).then_inc(s_wts, 16)
            act.dma_start(id_src[:, D:D + 1], a_l3[0:D, :]).then_inc(s_wts, 16)
            act.dma_start(id_src[:, D + 1:D + 2], a_l3[0:D, :]).then_inc(s_wts, 16)
            act.dma_start(a_dst[:, :], a_l3[D:2 * D, :]).then_inc(s_wts, 16)

            for mt in range(T):
                act.wait_ge(s_at_pe, mt + 1)
                nc.scalar.copy(AT[:, mt, :], banks[mt][:, :]).then_inc(s_at, 1)

            def layer0(i):
                for g in range(GROUPS0 - 1):
                    value_wait(act, s_l0_pe[0], GROUPS0 * i + g + 1)
                    bank = banks[g % 2]
                    step = (g - 1) % 4
                    if g == 0:
                        act.copy(vT_sb[0][:, :], bank[:, :]).then_inc(s_l0_ev[0], 1)
                    elif step == 0:
                        act.copy(eT_sb[0][:, :], bank[:, :]).then_inc(s_l0_ev[0], 1)
                    elif step == 1:
                        act.activation(hT_sb[0][:, :], bank[:, :], ACT.Relu, bias=b1_col[:, 0:1])\
                           .then_inc(s_l0_ev[0], 1)
                    elif step == 2:
                        act.activation(vT_sb[0][:, :], bank[:, :], ACT.Identity, bias=b2_col[:, 0:1])\
                           .then_inc(s_l0_ev[0], 1)
                    else:
                        act.copy(v_st[0][:, :, :], bank[:, :].rearrange("p (t c) -> p t c", t=T))\
                           .then_inc(s_l0_ev[0], 1)
            layer0(0)
            with act.Fori(1, B // 4) as i:
                layer0(i)

            def layernorm(j):
                act.wait_ge(s_ln[j], LN_CENTERED)
                act.activation(G[:, :], X[:, :, :].rearrange("p t c -> p (t c)"), ACT.Square).then_inc(s_ln[j], 1)
                act.wait_ge(s_ln[j], LN_VAR)
                act.activation(root[:, :], vare[:, :], ACT.Sqrt).then_inc(s_ln[j], 1)

            def transposed_x(j):
                def body(i):
                    for s in range(4):
                        value_wait(act, s_xt_pe[j], 4 * i + s + 1)
                        act.copy(XT[:, bass.ds((4 * i + s) * N, N)], banks[s][0:D, :]).then_inc(s_xt[j], 1)
                body(0)
                with act.Fori(1, B // 4) as i:
                    body(i)

            def attention(ph):
                kd = ph.k

                def body(i):
                    for k in range(8):
                        u, t = k // T, k % T
                        q, n = 2 * i + u, 8 * i + k
                        other = (u + 1) % 2
                        if ph.kind == "last" and exists(n, ph.tiles):
                            value_wait(act, ph.hn_pe, q + 1)
                            value_wait(act, ph.hb, q + 1)
                            value_wait(act, ph.lr, n - 1)
                            act.activation(t1[:, k % 2, :], banks[u][:, :], ACT.Identity,
                                           bias=hb[:, u, t, D:D + 1]).then_inc(ph.t1, 1)
                        if exists(n - 2, ph.tiles):
                            kp = (k - 2) % 8
                            value_wait(act, ph.T, n - 1)
                            value_wait(act, ph.AV, (q if t >= 2 else q - 1) - 1)
                            act.copy(pT[:, kp // T, :, (kp % T) * P:(kp % T + 1) * P],
                                     banks[2 + kp % 2][:, :].rearrange("p (m c) -> p m c", m=T)).then_inc(ph.PT, 1)
                        if ph.kind == "last":
                            if exists(n - 1, ph.tiles):
                                kp = (k - 1) % 8
                                value_wait(act, ph.neg, n)
                                value_wait(act, ph.T, n - 4)
                                value_wait(act, ph.rec, (q if t >= 1 else q - 1) - 1)
                                act.activation(pr[:, kp % 4, :], sc[:, kp % 4, :], ACT.Exp,
                                               bias=ng[:, kp % 4:kp % 4 + 1],
                                               accum_out=ls[:, kp // T, kp % T:kp % T + 1]).then_inc(ph.E, 1)
                        elif exists(n, ph.tiles):
                            value_wait(act, ph.neg, n + 1)
                            value_wait(act, ph.P, n - 3)
                            act.activation(ex[:, k % 4, :], sc[:, k % 4, :], ACT.Exp,
                                           bias=ng[:, k % 4:k % 4 + 1]).then_inc(ph.E, 1)
                        if t == 1 and exists(q + 1, ph.units):
                            value_wait(act, ph.h_pe, q + 2)
                            act.copy(hf[0:kd, other, :], banks[4][0:kd, :]).then_inc(ph.hf, 1)
                            if ph.kind != "last":
                                act.copy(hr[0:kd, other, :], banks[4][0:kd, :]).then_inc(ph.hr, 1)
                        if t == 3 and ph.kind == "heads" and exists(q - 1, ph.units):
                            value_wait(act, ph.AV, q)
                            value_wait(act, ph.z, q - 1)
                            act.activation(rel[:, :], banks[6][:, :], ACT.Relu, scale=0.99).then_inc(ph.rel, 1)
                iterations(act, ph.units, body)

            layernorm(0)
            transposed_x(0)
            attention(heads)
            attention(outer)
            act.wait_ge(s_deg, 1)
            act.activation(root[:, 0:T], deg[:, :], ACT.Sqrt).then_inc(s_deg, 1)
            layernorm(1)

            def layer2(i):
                for s in range(2):
                    value_wait(act, s_l2_pe[s], 2 * i + 1)
                    act.copy(eT_sb[s][:, :], banks[2 * s][:, :]).then_inc(s_l2_ev[s], 1)
            layer2(0)
            with act.Fori(1, B // 4) as i:
                layer2(i)
            layernorm(2)
            transposed_x(1)
            attention(last)
            layernorm(3)

        @block.tensor
        def _(pe):
            def transpose(to, of, parts=P):
                return pe.transpose(to, of, ident[0:parts, 0:parts])

            pe.wait_ge(s_id, 1)
            pe.wait_ge(s_adj, 16 * T)
            for mt in range(T):
                for t in range(T):
                    mm = transpose(banks[mt][:, t * P:(t + 1) * P], A[:, t, mt * P:(mt + 1) * P])
                mm.then_inc(s_at_pe, 1)
            pe.wait_ge(s_wts, 16 * N_WTS)
            for j in range(4):
                mm = transpose(banks[4][:, j * D:(j + 1) * D], w_dup[:, j, :, :].rearrange("p c k -> p (c k)"), D)
            mm.then_inc(s_wdup_pe, 1)
            pe.wait_ge(s_bd, 8)
            pe.wait_ge(s_at, T)

            def layer0(i):
                for g in range(GROUPS0):
                    for s in range(2):
                        bank = banks[2 * s + g % 2]
                        if g == 0:
                            value_wait(pe, s_l0_stage[s], i + 1)
                        else:
                            value_wait(pe, s_l0_ev[s], GROUPS0 * i + g)
                        step = (g - 1) % 4
                        if g == 0:
                            for t in range(T):
                                mm = transpose(bank[:, t * P:(t + 1) * P], v_st[s][:, t, :])
                        elif step == 0:
                            for m in range(T):
                                mm = pe.matmul(bank[:, :], v_st[s][:, m, :], AT[:, m, :],
                                               start=(m == 0), stop=(m == T - 1))
                        elif step == 1:
                            pe.matmul(bank[:, :], w_bd[:, 0, :], vT_sb[s][:, :], start=True, stop=False)
                            mm = pe.matmul(bank[:, :], w_bd[:, 1, :], eT_sb[s][:, :], start=False, stop=True)
                        elif step == 2:
                            mm = pe.matmul(bank[:, :], w_bd[:, 2, :], hT_sb[s][:, :], start=True, stop=True)
                        else:
                            for t in range(T):
                                mm = transpose(bank[:, t * P:(t + 1) * P], vT_sb[s][:, t * P:(t + 1) * P])
                        mm.then_inc(s_l0_pe[s], 1)
            layer0(0)
            with pe.Fori(1, B // 4) as i:
                layer0(i)
            for s in range(2):
                pe.wait_ge(s_l0_ev[s], GROUPS0 * B // 4)

            def transposed_x(j):
                def body(i):
                    for s in range(4):
                        value_wait(pe, s_xt_st[j], 4 * i + s + 1)
                        value_wait(pe, s_xt[j], 4 * i + s - 3)
                        pe.nop(nofuse=True)
                        for t in range(T):
                            mm = transpose(banks[s][0:D, t * P:(t + 1) * P], x_st[s][:, t, :])
                        mm.then_inc(s_xt_pe[j], 1)
                body(0)
                with pe.Fori(1, B // 4) as i:
                    body(i)
                pe.wait_ge(s_xt[j], B)

            def attention(ph):
                kd = ph.k

                def body(i):
                    for k in range(8):
                        u, t = k // T, k % T
                        q, n = 2 * i + u, 8 * i + k
                        other = (u + 1) % 2
                        if ph.kind != "last" and exists(n, ph.tiles):
                            value_wait(pe, ph.hr, q + 1)
                            value_wait(pe, ph.hl, q + 1)
                            value_wait(pe, ph.mx, n - 1)
                            a, b_ = hr[0:kd, u, t * P:(t + 1) * P], hl[0:kd, u, t * P:(t + 1) * P]
                            pe.matmul(banks[k % 2][:, :], a, hr[0:kd, u, :], start=True, stop=False)
                            pe.matmul(banks[k % 2][:, :], a, hl[0:kd, u, :], start=False, stop=False)
                            pe.matmul(banks[k % 2][:, :], b_, hr[0:kd, u, :], start=False, stop=True)\
                              .then_inc(ph.S, 1)
                        if exists(n - 2, ph.tiles):
                            kp = (k - 2) % 8
                            value_wait(pe, ph.E if ph.kind == "last" else ph.P, n - 1)
                            value_wait(pe, ph.PT, n - 3)
                            for m in range(T):
                                mm = transpose(banks[2 + kp % 2][:, m * P:(m + 1) * P],
                                               pr[:, kp % 4, m * P:(m + 1) * P])
                            mm.then_inc(ph.T, 1)
                        if t == 0 and exists(q + 1, ph.units):
                            if ph.kind == "heads":
                                value_wait(pe, ph.hr, q + 1)
                                head_mm(ph, i, u)
                            elif ph.kind == "outer":
                                value_wait(pe, ph.hr, q + 1)
                                value_wait(pe, ph.stage, q + 2)
                                pe.nop(nofuse=True)
                                for m in range(T):
                                    mm = transpose(banks[4][0:D, m * P:(m + 1) * P], x_st[0][:, m, :])
                                mm.then_inc(ph.h_pe, 1)
                            else:
                                value_wait(pe, ph.hf, q + 1)
                                pe.matmul(banks[4][:, :], W3_sb[:, :, :].rearrange("i c o -> i (c o)"),
                                          XT[:, bass.ds(batch_of(ph, i, u + 1) * N, N)],
                                          start=True, stop=True).then_inc(ph.h_pe, 1)
                        if t == 1 and ph.kind == "heads" and exists(q - 2, ph.units):
                            value_wait(pe, ph.z, q - 1)
                            value_wait(pe, ph.G, q - 2)
                            out_mm(ph, i, u)
                        if t == 2 and exists(q - 1, ph.units):
                            value_wait(pe, ph.PT, 4 * q)
                            value_wait(pe, ph.hb, q)
                            value_wait(pe, ph.z, q - 1)
                            if ph.kind == "heads":
                                for m in range(T):
                                    mm = pe.matmul(banks[6][:, :], hb[:, other, m, :], pT[:, other, m, :],
                                                   start=(m == 0), stop=(m == T - 1))
                            else:
                                for r in range(T):
                                    for m in range(T):
                                        mm = pe.matmul(banks[6][:, r * D:(r + 1) * D],
                                                       pT[:, other, m, r * P:(r + 1) * P], hb[:, other, m, 0:D],
                                                       start=(m == 0), stop=(m == T - 1))
                            mm.then_inc(ph.AV, 1)
                        if t == 3 and ph.kind != "outer" and exists(q + 1, ph.units):
                            value_wait(pe, ph.hf, q + 2)
                            value_wait(pe, ph.hb, q + 1)
                            if ph.kind == "heads":
                                for m in range(T):
                                    mm = transpose(banks[5][:, m * P:(m + 1) * P], hf[:, other, m * P:(m + 1) * P])
                            else:
                                for m in range(T):
                                    pe.matmul(banks[5][:, m * P:m * P + D + 2], hf[0:D, other, m * P:(m + 1) * P],
                                              id_src[:, :], start=True, stop=True)
                                value_wait(pe, ph.t1, 4 * q)
                                mm = pe.matmul(banks[other][:, :], a_dst_bc[:, :], hf[0:D, other, :],
                                               start=True, stop=True)
                            mm.then_inc(ph.hn_pe, 1)
                if ph.kind == "outer":
                    pe.wait_ge(heads.G, heads.units)
                if ph.kind == "last":
                    pe.wait_ge(s_adb, 3)
                iterations(pe, ph.units, body)

            def head_mm(ph, i, u):
                slot = (u + 1) % 2
                pe.wait_ge(s_wh[slot], 16 * (i + 1 + u))
                pe.matmul(banks[4][:, :], wh_slot[slot][:, :], XT[:, bass.ds(batch_of(ph, i, u + 1) * N, N)],
                          start=True, stop=True).then_inc(ph.h_pe, 1)

            def out_mm(ph, i, u):
                pe.wait_ge(s_wo[u], 16 * i)
                for m in range(T):
                    mm = pe.matmul(banks[7][:, m * D:(m + 1) * D], z[:, m * P:(m + 1) * P], wo_slot[u][:, :],
                                   start=True, stop=True)
                mm.then_inc(ph.G_pe, 1)

            transposed_x(0)
            attention(heads)
            attention(outer)

            def layer2(i):
                for s in range(2):
                    value_wait(pe, s_l2_stage[s], i + 1)
                    value_wait(pe, s_l2_ev[s], 2 * i)
                    for m in range(T):
                        mm = pe.matmul(banks[2 * s][:, :], v_st[s][:, m, :], AT[:, m, :],
                                       start=(m == 0), stop=(m == T - 1))
                    mm.then_inc(s_l2_pe[s], 1)
                for s in range(2):
                    value_wait(pe, s_l2_ev[s], 2 * i + 1)
                    for t in range(T):
                        mm = pe.matmul(banks[2 * s + 1][:, t * P:(t + 1) * P], eT_sb[s][:, t * P:(t + 1) * P],
                                       w_bd[:, 3, :], start=True, stop=True)
                    mm.then_inc(s_l2_pe[s], 1)
            pe.wait_ge(s_deg2, 1 + T)
            pe.wait_ge(outer.z, outer.units)
            layer2(0)
            with pe.Fori(1, B // 4) as i:
                layer2(i)
            for s in range(2):
                pe.wait_ge(s_l2_ev[s], 2 * B // 4)
            transposed_x(1)
            attention(last)

        @block.vector
        def _(dve):
            dve.wait_ge(s_wdup_pe, 1)
            dve.wait_ge(s_bd0, 1)
            for j in range(4):
                for c in range(2):
                    dve.tensor_copy(w_bd[c * D:(c + 1) * D, j, c * D:(c + 1) * D],
                                    banks[4][c * D:(c + 1) * D, j * D:(j + 1) * D]).then_inc(s_bd, 1)
            dve.tensor_copy(a_dst_bc[:, :], a_dst[:, 0:1].to_broadcast([D, P])).then_inc(s_adb, 1)
            dve.wait_ge(s_id, 1)
            dve.tensor_copy(id_src[:, 0:D], ident[0:D, 0:D]).then_inc(s_adb, 1)
            dve.memset(zeros[:, :], 0.0).then_inc(s_adb, 1)

            def layer0(i):
                for g in range(GROUPS0):
                    step = (g - 1) % 4
                    for s in range(2):
                        bank = banks[2 * s + g % 2]
                        if s == 0 and g < GROUPS0 - 1:
                            continue
                        value_wait(dve, s_l0_pe[s], GROUPS0 * i + g + 1)
                        if g == 0:
                            mm = dve.tensor_copy(vT_sb[s][:, :], bank[:, :])
                        elif step == 0:
                            mm = dve.tensor_copy(eT_sb[s][:, :], bank[:, :])
                        elif step == 1:
                            mm = dve.tensor_scalar(hT_sb[s][:, :], bank[:, :], b1_col[:, 0:1], 0.0,
                                                   ALU.add, ALU.max)
                        elif step == 2:
                            mm = dve.tensor_scalar(vT_sb[s][:, :], bank[:, :], b2_col[:, 0:1], None, ALU.add)
                        elif g < GROUPS0 - 1:
                            mm = dve.tensor_copy(v_st[s][:, :, :], bank[:, :].rearrange("p (t c) -> p t c", t=T))
                        else:
                            xs = X[:, :, bass.ds((2 * i + s) * 2 * D, 2 * D)]
                            mm = dve.tensor_tensor(xs, bank[:, :].rearrange("p (t c) -> p t c", t=T), xs, ALU.add)
                        mm.then_inc(s_l0_ev[s], 1)
            dve.wait_ge(s_x, 16 * T)
            layer0(0)
            with dve.Fori(1, B // 4) as i:
                layer0(i)

            def layernorm(j):
                sm = s_ln[j]
                count = [0]

                def step(ins):
                    count[0] += 1
                    ins.then_inc(sm, 1)
                    dve.wait_ge(sm, count[0])

                x3 = X[:, :, :].rearrange("p t (b d) -> p (t b) d", d=D)
                g3 = G[:, :].rearrange("p (g d) -> p g d", d=D)
                per_node = lambda a: a[:, :].unsqueeze(2).to_broadcast([P, GR, D])
                step(dve.tensor_reduce(mean[:, :], x3, AX.X, ALU.add))
                step(dve.tensor_scalar(mean[:, :], mean[:, :], -1.0 / D, None, ALU.mult))
                step(dve.tensor_tensor(x3, x3, per_node(mean), ALU.add))
                count[0] += 1
                dve.wait_ge(sm, count[0])
                step(dve.tensor_reduce(vare[:, :], g3, AX.X, ALU.add))
                step(dve.tensor_scalar(vare[:, :], vare[:, :], 1.0 / D, LN_EPS, ALU.mult, ALU.add))
                count[0] += 1
                dve.wait_ge(sm, count[0])
                step(dve.reciprocal(rstd[:, :], root[:, :]))
                step(dve.tensor_tensor(newt[:, :], rstd[:, :], rstd[:, :], ALU.mult))
                step(dve.tensor_tensor(newt[:, :], newt[:, :], vare[:, :], ALU.mult))
                step(dve.tensor_scalar(newt[:, :], newt[:, :], -0.5, 1.5, ALU.mult, ALU.add))
                step(dve.tensor_tensor(rstd[:, :], rstd[:, :], newt[:, :], ALU.mult))
                step(dve.tensor_tensor(x3, x3, per_node(rstd), ALU.mult))

            def attention(ph):
                def body(i):
                    for k in range(8):
                        u, t = k // T, k % T
                        q, n = 2 * i + u, 8 * i + k
                        other = (u + 1) % 2
                        if exists(n, ph.tiles):
                            if ph.kind == "last":
                                value_wait(dve, ph.t1, n + 1)
                                value_wait(dve, ph.mx, n - 1)
                                dve.scalar_tensor_tensor(out=lr[:, k % 2, :], in0=t1[:, k % 2, :], scalar=0.2,
                                                         in1=t1[:, k % 2, :], op0=ALU.mult, op1=ALU.max)\
                                   .then_inc(ph.lr, 1)
                                value_wait(dve, ph.lr, n + 1)
                                value_wait(dve, ph.E, n - 3)
                                src, weight = lr[:, k % 2, :], A1[:, t, :]
                            else:
                                value_wait(dve, ph.S, n + 1)
                                value_wait(dve, ph.P, n - 3)
                                src, weight = banks[k % 2][:, :], A[:, t, :]
                            dve.nop(nofuse=True)
                            dve.tensor_tensor_reduce(sc[:, k % 4, :], src, weight, 1.0, LOWEST, ALU.mult, ALU.max,
                                                     mx[:, k % 4:k % 4 + 1]).then_inc(ph.mx, 1)
                        if ph.kind != "last" and exists(n - 1, ph.tiles):
                            kp = (k - 1) % 8
                            value_wait(dve, ph.E, n)
                            value_wait(dve, ph.T, n - 4)
                            value_wait(dve, ph.rec, (q if t >= 1 else q - 1) - 1)
                            dve.scalar_tensor_tensor(out=pr[:, kp % 4, :], in0=sc[:, kp % 4, :],
                                                     scalar=cc[:, kp % 4:kp % 4 + 1], in1=ex[:, kp % 4, :],
                                                     op0=ALU.not_equal, op1=ALU.mult,
                                                     accum_out=ls[:, kp // T, kp % T:kp % T + 1]).then_inc(ph.P, 1)
                        if t == 1 and exists(q - 1, ph.units):
                            value_wait(dve, ph.E if ph.kind == "last" else ph.P, 4 * q)
                            value_wait(dve, ph.G if ph.kind == "heads" else ph.z, q - 2)
                            dve.reciprocal(rc[:, other, :], ls[:, other, :]).then_inc(ph.rec, 1)
                        if t == 2 and ph.kind == "heads" and exists(q - 2, ph.units):
                            value_wait(dve, ph.G_pe, q - 1)
                            value_wait(dve, ph.G, q - 2)
                            value_wait(dve, ph.rec, q - 1)
                            for m in range(T):
                                gs = G[:, bass.ds(batch_of(ph, i - 1, u) * T * D + m * D, D)]
                                ins = dve.scalar_tensor_tensor(out=gs, in0=banks[7][:, m * D:(m + 1) * D],
                                                               scalar=rc[:, u, m:m + 1], in1=gs,
                                                               op0=ALU.mult, op1=ALU.add)
                            ins.then_inc(ph.G, 1)
                        if t == 3 and exists(q - 1, ph.units):
                            if ph.kind == "heads":
                                value_wait(dve, ph.rel, q)
                                value_wait(dve, ph.G_pe, q - 1)
                                dve.scalar_tensor_tensor(out=z[:, :], in0=banks[6][:, :], scalar=0.01,
                                                         in1=rel[:, :], op0=ALU.mult, op1=ALU.add)\
                                   .then_inc(ph.z, 1)
                            else:
                                value_wait(dve, ph.AV, q)
                                value_wait(dve, ph.rec, q)
                                value_wait(dve, ph.z, q - 1)
                                bias = bo_bc if ph.kind == "outer" else bias3_bc
                                for m in range(T):
                                    ins = dve.scalar_tensor_tensor(out=y[:, m, :], in0=banks[6][:, m * D:(m + 1) * D],
                                                                   scalar=rc[:, other, m:m + 1], in1=bias[:, :],
                                                                   op0=ALU.mult, op1=ALU.add)
                                ins.then_inc(ph.y, 1)
                                xs = X[:, :, bass.ds(batch_of(ph, i, u - 1) * D, D)]
                                res = y
                                if ph.kind == "outer":
                                    value_wait(dve, ph.y, 2 * q - 1)
                                    dve.scalar_tensor_tensor(out=y2[:, :, :], in0=y[:, :, :], scalar=0.01,
                                                             in1=y[:, :, :], op0=ALU.mult, op1=ALU.max)\
                                       .then_inc(ph.y, 1)
                                    value_wait(dve, ph.y, 2 * q)
                                    res = y2
                                else:
                                    value_wait(dve, ph.y, q)
                                dve.tensor_tensor(xs, xs, res[:, :, :], ALU.add).then_inc(ph.z, 1)
                        if t == 3 and exists(q + 1, ph.units):
                            value_wait(dve, ph.AV, q)
                            if ph.kind == "heads":
                                value_wait(dve, ph.hn_pe, q + 2)
                                hb_head(ph, i, u)
                            elif ph.kind == "outer":
                                dve.tensor_copy(hb[:, other, :, 0:D],
                                                G[:, bass.ds(batch_of(ph, i, u + 1) * T * D, T * D)]
                                                .rearrange("p (t d) -> p t d", t=T)).then_inc(ph.hb, 1)
                            else:
                                value_wait(dve, ph.hn_pe, q + 2)
                                dve.tensor_copy(hb[:, other, :, 0:D + 2],
                                                banks[5][:, :].rearrange("p (t c) -> p t c", t=T)[:, :, 0:D + 2])\
                                   .then_inc(ph.hb, 1)
                iterations(dve, ph.units, body)

            def hb_head(ph, i, u):
                slot = (u + 1) % 2
                dve.wait_ge(s_bb[slot], 16 * (i + 1 + u))
                dve.tensor_tensor(hb[:, slot, :, :], banks[5][:, :].rearrange("p (t c) -> p t c", t=T),
                                  bb_slot[slot][:, :].unsqueeze(1).to_broadcast([P, T, HID]),
                                  ALU.add).then_inc(ph.hb, 1)

            for s in range(2):
                dve.wait_ge(s_l0_ev[s], GROUPS0 * B // 4)
            layernorm(0)
            dve.wait_ge(s_adj, 16 * T)
            dve.memset(G[:, :], 0.0).then_inc(s_gz, 1)
            dve.wait_ge(s_gz, 1)
            attention(heads)
            dve.wait_ge(heads.G, heads.units)
            attention(outer)
            dve.wait_ge(outer.z, outer.units)

            dve.tensor_reduce(deg[:, :], A[:, :, :], AX.X, ALU.add).then_inc(s_deg2, 1)
            dve.wait_ge(s_deg2, 1)
            dve.tensor_scalar(deg[:, :], deg[:, :], 1.0, None, ALU.add).then_inc(s_deg, 1)
            for t in range(T):
                blk = AT[:, t, t * P:(t + 1) * P]
                dve.tensor_tensor(blk, blk, ident[:, :], ALU.add).then_inc(s_deg2, 1)
            dve.wait_ge(s_deg, 2)

            def step2(ins, n):
                ins.then_inc(s_deg, 1)
                dve.wait_ge(s_deg, n)
            step2(dve.reciprocal(dinv[:, :], root[:, 0:T]), 3)
            step2(dve.tensor_tensor(newt[:, 0:T], dinv[:, :], dinv[:, :], ALU.mult), 4)
            step2(dve.tensor_tensor(newt[:, 0:T], newt[:, 0:T], deg[:, :], ALU.mult), 5)
            step2(dve.tensor_scalar(newt[:, 0:T], newt[:, 0:T], -0.5, 1.5, ALU.mult, ALU.add), 6)
            step2(dve.tensor_tensor(dinv[:, :], dinv[:, :], newt[:, 0:T], ALU.mult), 7)
            layernorm(1)

            def layer2(i):
                for s in range(2):
                    value_wait(dve, s_l2_pe[s], 2 * i - 1)
                    for t in range(T):
                        ins = dve.tensor_scalar(v_st[s][:, t, :], X[:, t, bass.ds((2 * i + s) * 2 * D, 2 * D)],
                                                dinv[:, t:t + 1], None, ALU.mult)
                    ins.then_inc(s_l2_stage[s], 1)
                for s in range(2):
                    value_wait(dve, s_l2_pe[s], 2 * i + 2)
                    for t in range(T):
                        xs = X[:, t, bass.ds((2 * i + s) * 2 * D, 2 * D)]
                        ins = dve.scalar_tensor_tensor(out=xs, in0=banks[2 * s + 1][:, t * P:(t + 1) * P],
                                                       scalar=dinv[:, t:t + 1], in1=xs, op0=ALU.mult, op1=ALU.add)
                    ins.then_inc(s_l2_ev[s], 1)
            layer2(0)
            with dve.Fori(1, B // 4) as i:
                layer2(i)
            for s in range(2):
                dve.wait_ge(s_l2_ev[s], 2 * B // 4)
            layernorm(2)
            dve.wait_ge(s_a1, T)
            attention(last)
            dve.wait_ge(last.z, last.units)
            layernorm(3)


_INS = ["x", "adj", "L0_gnn_intervention_value", "L0_gnn_W1", "L0_gnn_b1", "L0_gnn_W2", "L0_gnn_b2",
        "L1_gnn_Wh", "L1_gnn_bh", "L1_gnn_W_out", "L1_gnn_b_out", "L2_gnn_W",
        "L3_gnn_weight", "L3_gnn_a", "L3_gnn_bias"]
_OUTS = [((B, N, D), "float32")]


def kernel(**inputs):
    import numpy as _np
    import concourse.bacc as _bacc
    from concourse import mybir as _mybir
    from concourse.bass_utils import run_bass_kernel_spmd as _run

    nc = _bacc.Bacc("TRN2", target_bir_lowering=False, num_devices=1)
    arrays, args = {}, []
    for name in _INS:
        a = _np.ascontiguousarray(inputs[name])
        arrays[f"in_{name}_dram"] = a
        args.append(nc.dram_tensor(f"in_{name}_dram", a.shape, _mybir.dt.from_np(a.dtype), kind="ExternalInput").ap())
    for i, (shape, dtype) in enumerate(_OUTS):
        dt = _mybir.dt.from_np(_np.dtype(dtype))
        args.append(nc.dram_tensor(f"out_{i}_dram", shape, dt, kind="ExternalOutput").ap())
    gnn_stack_program(nc, *args)
    r = _run(nc, [arrays], core_ids=[0])
    return r.results[0]["out_0_dram"]
```

```python
from contextlib import ExitStack

import concourse.bass as bass
from concourse import mybir

ALU = mybir.AluOpType
ACT = mybir.ActivationFunctionType
AX = mybir.AxisListType
F32 = mybir.dt.float32
F32R = mybir.dt.float32r
I32 = mybir.dt.int32

P = 128
B = 16
N = 512
D = 64
T = N // P
HEADS = 8
HID = 128
LN_EPS = 1e-5
SLOTS = 4
LAG = 3
LOWEST = -3.0e38


def value_wait(engine, semaphore, value):
    if not (isinstance(value, int) and value <= 0):
        engine.wait_ge(semaphore, value)


def exists(index, total):
    return 0 <= index < total if isinstance(index, int) else True


def gnn_stack_program(nc, x, adj, iv, W1, b1, W2, b2, Wh, bh, Wo, bo, W_l2, W_l3, a_l3, bias_l3, out):
    with ExitStack() as ctx:
        def sb(name, shape, dt=F32):
            return ctx.enter_context(nc.sbuf_tensor(name, shape, dt))

        def sem(name):
            return ctx.enter_context(nc.semaphore(name))

        X = sb("X", [P, T, B * D])
        G = sb("G", [P, B * T * D])
        V = G[:, :].rearrange("p (t c) -> p t c", t=T)
        XT = sb("XT", [P, B * N], F32R)
        A = sb("A", [P, T, N])
        AT = sb("AT", [P, T, N])
        AT_hi = sb("AT_hi", [P, T, N], F32R)
        AT_lo = sb("AT_lo", [P, T, N], F32R)
        ident = sb("ident", [P, P])
        zeros = sb("zeros", [P, 1])
        w_dup = sb("w_dup", [D, 4, 2, D])
        w_bd = sb("w_bd", [P, 4, P])
        b1_col = sb("b1_col", [P, 1])
        b2_col = sb("b2_col", [P, 1])
        wh_slot = [sb(f"wh_slot{s}", [P, HID]) for s in range(2)]
        wh_hi = [sb(f"wh_hi{s}", [P, HID], F32R) for s in range(2)]
        wh_lo = [sb(f"wh_lo{s}", [P, HID], F32R) for s in range(2)]
        bb_slot = [sb(f"bb_slot{s}", [P, HID]) for s in range(2)]
        wo_slot = [sb(f"wo_slot{s}", [P, D]) for s in range(2)]
        bo_bc = sb("bo_bc", [P, D])
        W3_sb = sb("W3_sb", [P, 2, D])
        W3_hi = sb("W3_hi", [P, 2, D], F32R)
        W3_lo = sb("W3_lo", [P, 2, D], F32R)
        a_src = sb("a_src", [D, 2])
        a_dst = sb("a_dst", [D, 1])
        a_dst_bc = sb("a_dst_bc", [D, P])
        bias3_bc = sb("bias3_bc", [P, D])
        v_st = [sb(f"v_st{s}", [P, T, 2 * D]) for s in range(SLOTS)]
        v_hi = [sb(f"v_hi{s}", [P, T, 2 * D], F32R) for s in range(SLOTS)]
        v_lo = [sb(f"v_lo{s}", [P, T, 2 * D], F32R) for s in range(SLOTS)]
        GR = T * B
        mean = sb("mean", [P, GR])
        vare = sb("vare", [P, GR])
        root = sb("root", [P, GR])
        rstd = sb("rstd", [P, GR])
        newt = sb("newt", [P, GR])
        newt2 = sb("newt2", [P, GR])
        deg = sb("deg", [P, T])
        dinv = sb("dinv", [P, T])
        x_st = [sb(f"x_st{s}", [P, T, 2, D], F32R) for s in range(4)]
        g_st = sb("g_st", [P, T, D])
        hf = sb("hf", [P, 2, N])
        hr = sb("hr", [P, 2, N], F32R)
        hl = sb("hl", [P, 2, N], F32R)
        hb = sb("hb", [P, 2, T, HID])
        sc = sb("sc", [P, 4, N])
        ex = sb("ex", [P, 4, N])
        pr = sb("pr", [P, 4, N])
        pT = sb("pT", [P, 2, T, N])
        t1, lr = ex[:, 0:2, :], ex[:, 2:4, :]
        es = sb("es", [P, 2, T, 2])
        vT_sb = [ex[:, s, :] for s in range(SLOTS)]
        eT_sb = [sc[:, s, :] for s in range(SLOTS)]
        hT_sb = [pr[:, s, :] for s in range(SLOTS)]
        rel = sb("rel", [P, N])
        z = sb("z", [P, N])
        mx = sb("mx", [P, 4])
        ng = sb("ng", [P, 4])
        cc = sb("cc", [P, 4])
        ls = sb("ls", [P, 2, T])
        rc = sb("rc", [P, 2, T])
        y = sb("y", [P, T, D])
        y2 = sb("y2", [P, T, D])

        banks = [ctx.enter_context(nc.psum_tensor(f"bank{i}", [P, N], F32)) for i in range(8)]

        s_x = sem("s_x")
        s_v = sem("s_v")
        s_iv = sem("s_iv")
        s_adj = sem("s_adj")
        s_wts = sem("s_wts")
        s_ones = sem("s_ones")
        s_wdup_pe = sem("s_wdup_pe")
        s_bd0 = sem("s_bd0")
        s_bd = sem("s_bd")
        s_idp = sem("s_idp")
        s_id = sem("s_id")
        s_a1 = sem("s_a1")
        s_at_pe = sem("s_at_pe")
        s_at = sem("s_at")
        s_adb = sem("s_adb")
        s_l0_stage = [sem(f"s_l0_stage{s}") for s in range(SLOTS)]
        s_l0_pe = [sem(f"s_l0_pe{s}") for s in range(SLOTS)]
        s_l0_ev = [sem(f"s_l0_ev{s}") for s in range(SLOTS)]
        s_deg = sem("s_deg")
        s_l2_stage = [sem(f"s_l2_stage{s}") for s in range(SLOTS)]
        s_l2_pe = [sem(f"s_l2_pe{s}") for s in range(SLOTS)]
        s_l2_ev = [sem(f"s_l2_ev{s}") for s in range(SLOTS)]
        s_ln = [sem(f"s_ln{j}") for j in range(4)]
        s_xt_st = [sem(f"s_xt_st{j}") for j in range(2)]
        s_xt_pe = [sem(f"s_xt_pe{j}") for j in range(2)]
        s_xt = [sem(f"s_xt{j}") for j in range(2)]
        s_out = sem("s_out")

        s_wh = [sem(f"s_wh{s}") for s in range(2)]
        s_bb = [sem(f"s_bb{s}") for s in range(2)]
        s_wo = [sem(f"s_wo{s}") for s in range(2)]
        s_gz = sem("s_gz")
        s_w3 = sem("s_w3")
        s_at_hi = sem("s_at_hi")
        s_at_lo = sem("s_at_lo")
        s_at2_hi = sem("s_at2_hi")
        s_at2_lo = sem("s_at2_lo")
        s_l0_sthi = [sem(f"s_l0_sthi{s}") for s in range(SLOTS)]
        s_l0_hi = [sem(f"s_l0_hi{s}") for s in range(SLOTS)]
        s_l2_x = [sem(f"s_l2_x{s}") for s in range(SLOTS)]
        s_l2_hi = [sem(f"s_l2_hi{s}") for s in range(SLOTS)]
        s_xt_hi = [sem(f"s_xt_hi{j}") for j in range(2)]
        s_deg2 = sem("s_deg2")

        N_WTS = 8 + 4 + 9
        LN_CENTERED, LN_VAR, LN_STEPS, DEG_STEPS = 3, 6, 13, 7
        STEPS = 3
        GROUPS0 = 1 + 4 * STEPS

        class AttentionPhase:

            def __init__(self, kind, units, k):
                self.kind, self.units, self.tiles, self.k = kind, units, units * T, k
                self.h_pe = sem(f"{kind}_h_pe")
                self.hf = sem(f"{kind}_hf")
                self.hb = sem(f"{kind}_hb")
                self.mx = sem(f"{kind}_mx")
                self.neg = sem(f"{kind}_neg")
                self.E = sem(f"{kind}_E")
                self.T = sem(f"{kind}_T")
                self.PT = sem(f"{kind}_PT")
                self.rec = sem(f"{kind}_rec")
                self.AV = sem(f"{kind}_AV")
                self.z = sem(f"{kind}_z")
                if kind != "last":
                    self.stage = sem(f"{kind}_stage")
                    self.hr = sem(f"{kind}_hr")
                    self.hl = sem(f"{kind}_hl")
                    self.S = sem(f"{kind}_S")
                    self.cc = sem(f"{kind}_cc")
                    self.P = sem(f"{kind}_P")
                if kind != "outer":
                    self.hn_pe = sem(f"{kind}_hn_pe")
                if kind != "heads":
                    self.y = sem(f"{kind}_y")
                if kind == "heads":
                    self.wh = sem(f"{kind}_wh")
                    self.rel = sem(f"{kind}_rel")
                    self.G_pe = sem(f"{kind}_G_pe")
                    self.G = sem(f"{kind}_G")
                if kind == "last":
                    self.es_pe = sem(f"{kind}_es_pe")
                    self.es = sem(f"{kind}_es")
                    self.t1 = sem(f"{kind}_t1")
                    self.lr = sem(f"{kind}_lr")

        heads = AttentionPhase("heads", B * HEADS, HID)
        outer = AttentionPhase("outer", B, D)
        last = AttentionPhase("last", B, D)

        def iterations(engine, units, body):
            pairs = units // 2
            for i in (-1, 0, 1):
                body(i)
            with engine.Fori(2, pairs - 1) as i:
                body(i)
            for i in (pairs - 1, pairs, pairs + 1):
                body(i)

        def batch_of(ph, i, unit_in_pair):
            carry, u = divmod(unit_in_pair, 2)
            return (i + carry) % B if ph.kind == "heads" else 2 * (i + carry) + u

        block = ctx.enter_context(nc.Block())

        @block.sync
        def _(sp):
            for t in range(T):
                sp.dma_start(A[:, t, :], adj[t * P:(t + 1) * P, :]).then_inc(s_adj, 16)
            for t in range(T):
                sp.dma_start(V[:, t, :].rearrange("p (b d) -> p b d", b=B),
                             x[:, t * P:(t + 1) * P, :].rearrange("b p d -> p b d")).then_inc(s_v, 16)
            sp.wait_ge(s_v, 16 * T)
            for b in range(B):
                sp.dma_start(V[0:1, 0, b * D:(b + 1) * D], iv).then_inc(s_iv, 16)
            for t in range(T):
                sp.dma_start(X[:, t, :].rearrange("p (b d) -> p b d", b=B),
                             x[:, t * P:(t + 1) * P, :].rearrange("b p d -> p b d")).then_inc(s_x, 16)

            pairs = B * HEADS // 2

            def load_split_weights(i, u):
                if exists(i, pairs):
                    value_wait(sp, heads.wh, 2 * i + u - 1)
                    for c in range(2):
                        sp.dma_start(wh_slot[u][c * D:(c + 1) * D, :], Wh[bass.ds(i // B * 2 + u, 1), :, :]
                                     .rearrange("a i o -> (a i) o")).then_inc(s_wh[u], 16)

            def load_bias(i, u):
                if exists(i, pairs):
                    value_wait(sp, heads.hb, 2 * i + u - 1)
                    sp.dma_start(bb_slot[u][:, :], bh[bass.ds(i // B * 2 + u, 1), :].to_broadcast([P, HID]))\
                      .then_inc(s_bb[u], 16)

            def load_projection(i, u):
                if exists(i, pairs):
                    value_wait(sp, heads.G_pe, 2 * i + u - 1)
                    sp.dma_start(wo_slot[u][:, :], Wo[bass.ds((i // B * 2 + u) * HID, HID), :])\
                      .then_inc(s_wo[u], 16)

            def head_weights(i):
                load_split_weights(i, 0)
                load_projection(i - 2, 0)
                load_projection(i - 2, 1)
                load_bias(i, 0)
                load_split_weights(i, 1)
                load_bias(i, 1)

            for i in (0, 1, 2):
                head_weights(i)
            with sp.Fori(3, pairs) as i:
                head_weights(i)
            for i in (pairs, pairs + 1):
                head_weights(i)

            sp.wait_ge(s_ln[3], LN_STEPS)
            for t in range(T):
                sp.dma_start(out[:, t * P:(t + 1) * P, :].rearrange("b p d -> p b d"),
                             X[:, t, :].rearrange("p (b d) -> p b d", b=B)).then_inc(s_out, 16)
            sp.wait_ge(s_out, 16 * T)

        @block.gpsimd
        def _(pool):
            def after_wait():
                pool.nop(nofuse=True)

            nc.gpsimd.memset(ident[:, :], 0.0).then_inc(s_idp, 1)
            nc.gpsimd.memset(w_bd[:, :, :], 0.0).then_inc(s_bd0, 1)
            pool.wait_ge(s_idp, 1)
            nc.gpsimd.affine_select(out=ident[:, :], in_=ident[:, :], compare_op=ALU.not_equal, fill=1.0,
                                    base=0, pattern=[[-1, P]], channel_multiplier=1).then_inc(s_id, 1)
            pool.wait_ge(s_wts, 16 * N_WTS)
            pool.tensor_copy(W3_hi[:, :, :], W3_sb[:, :, :]).then_inc(s_w3, 1)
            pool.wait_ge(s_w3, 1)
            pool.tensor_tensor(W3_lo[:, :, :], W3_sb[:, :, :], W3_hi[:, :, :].bitcast(F32),
                               ALU.subtract).then_inc(s_w3, 1)

            pool.wait_ge(s_iv, 16 * B)
            for i in range(B // 2 // SLOTS):
                for s in range(SLOTS):
                    vs = V[:, :, (SLOTS * i + s) * 2 * D:(SLOTS * i + s + 1) * 2 * D]
                    value_wait(pool, s_l0_pe[s], GROUPS0 * i - 3)
                    pool.tensor_copy(v_hi[s][:, :, :], vs).then_inc(s_l0_sthi[s], 1)
                    pool.wait_ge(s_l0_sthi[s], i + 1)
                    pool.tensor_tensor(v_lo[s][:, :, :], vs, v_hi[s][:, :, :].bitcast(F32),
                                       ALU.subtract).then_inc(s_l0_stage[s], 1)

            def attention(ph):
                def body(i):
                    for k in range(8):
                        u, t = k // T, k % T
                        q, n = 2 * i + u, 8 * i + k
                        other = (u + 1) % 2
                        if exists(n, ph.tiles):
                            value_wait(pool, ph.mx, n + 1)
                            value_wait(pool, ph.E if ph.kind == "last" else ph.P, n - 3)
                            after_wait()
                            slot = slice(k % 4, k % 4 + 1)
                            pool.tensor_scalar(ng[:, slot], mx[:, slot], -1.0, None, ALU.mult).then_inc(ph.neg, 1)
                            if ph.kind != "last":
                                pool.tensor_scalar(cc[:, slot], mx[:, slot], 0.0, None, ALU.is_equal)\
                                    .then_inc(ph.cc, 1)
                        if t == 2 and ph.kind != "last" and exists(q + 1, ph.units):
                            value_wait(pool, ph.hr, q + 2)
                            after_wait()
                            pool.tensor_tensor(hl[0:ph.k, other, :], hf[0:ph.k, other, :],
                                               hr[0:ph.k, other, :].bitcast(F32), ALU.subtract).then_inc(ph.hl, 1)
                        if t == 2 and ph.kind == "outer" and exists(q + 2, ph.units):
                            value_wait(pool, ph.h_pe, q + 2)
                            after_wait()
                            pool.tensor_copy(g_st[:, :, :], G[:, bass.ds(batch_of(ph, i, u + 2) * T * D, T * D)]
                                             .rearrange("p (t d) -> p t d", t=T)).then_inc(ph.stage, 1)
                        if t == 3 and ph.kind == "heads" and exists(q + 2, ph.units):
                            value_wait(pool, s_wh[u], 32 * (i + 2))
                            value_wait(pool, ph.h_pe, q + 1)
                            after_wait()
                            pool.tensor_copy(wh_hi[u][:, :], wh_slot[u][:, :]).then_inc(ph.stage, 1)
                            value_wait(pool, ph.stage, q + 3)
                            after_wait()
                            pool.tensor_tensor(wh_lo[u][:, :], wh_slot[u][:, :], wh_hi[u][:, :].bitcast(F32),
                                               ALU.subtract).then_inc(ph.wh, 1)
                if ph.kind == "outer":
                    pool.wait_ge(heads.G, heads.units)
                iterations(pool, ph.units, body)

            def low_half_x(j):
                def body(i):
                    for s in range(4):
                        value_wait(pool, s_xt_hi[j], 4 * i + s + 1)
                        after_wait()
                        pool.tensor_tensor(x_st[s][:, :, 1, :], X[:, :, bass.ds((4 * i + s) * D, D)],
                                           x_st[s][:, :, 0, :].bitcast(F32), ALU.subtract).then_inc(s_xt_st[j], 1)
                body(0)
                with pool.Fori(1, B // 4) as i:
                    body(i)

            low_half_x(0)
            attention(heads)
            attention(outer)

            for i in range(B // 2 // SLOTS):
                for s in range(SLOTS):
                    pool.wait_ge(s_l2_hi[s], i + 1)
                    pool.tensor_tensor(v_lo[s][:, :, :], v_st[s][:, :, :], v_hi[s][:, :, :].bitcast(F32),
                                       ALU.subtract).then_inc(s_l2_stage[s], 1)
            pool.wait_ge(s_deg2, 1)
            for t in range(T):
                nc.gpsimd.affine_select(out=A[:, t, :], in_=A[:, t, :], compare_op=ALU.not_equal, fill=1.0,
                                        base=t * P, pattern=[[-1, N]], channel_multiplier=1).then_inc(s_a1, 1)
            low_half_x(1)
            attention(last)

        @block.scalar
        def _(act):
            for j, w in enumerate((W1[:, 0:D], W1[:, D:2 * D], W2, W_l2)):
                for c in range(2):
                    act.dma_start(w_dup[:, j, c, :], w).then_inc(s_wts, 16)
            for c in range(2):
                act.dma_start(b1_col[c * D:(c + 1) * D, :], b1.rearrange("(p a) -> p a", a=1)).then_inc(s_wts, 16)
                act.dma_start(b2_col[c * D:(c + 1) * D, :], b2.rearrange("(p a) -> p a", a=1)).then_inc(s_wts, 16)
            act.dma_start(bo_bc[:, :], bo.partition_broadcast(P)).then_inc(s_wts, 16)
            act.dma_start(bias3_bc[:, :], bias_l3.partition_broadcast(P)).then_inc(s_wts, 16)
            for c in range(2):
                for r in range(2):
                    act.dma_start(W3_sb[r * D:(r + 1) * D, c, :], W_l3).then_inc(s_wts, 16)
                act.dma_start(a_src[:, c:c + 1], a_l3[0:D, :]).then_inc(s_wts, 16)
            act.dma_start(a_dst[:, :], a_l3[D:2 * D, :]).then_inc(s_wts, 16)

            for mt in range(T):
                act.wait_ge(s_at_pe, mt + 1)
                nc.scalar.copy(AT[:, mt, :], banks[mt][:, :]).then_inc(s_at, 1)
                nc.scalar.copy(AT_hi[:, mt, :], banks[mt][:, :]).then_inc(s_at_hi, 1)

            for i in range(B // 2 // SLOTS):
                for g in range(GROUPS0 - 1):
                    step = (g - 1) % 4
                    for s in range(SLOTS):
                        value = g > 0 and step == 3
                        if s % 2 and not value:
                            continue
                        act.wait_ge(s_l0_pe[s], GROUPS0 * i + g + 1)
                        bank = banks[2 * s + g % 2]
                        if g == 0:
                            act.copy(vT_sb[s], bank[:, :]).then_inc(s_l0_ev[s], 1)
                        elif step == 0:
                            act.copy(eT_sb[s], bank[:, :]).then_inc(s_l0_ev[s], 1)
                        elif step == 1:
                            act.activation(hT_sb[s], bank[:, :], ACT.Relu, bias=b1_col[:, 0:1])\
                               .then_inc(s_l0_ev[s], 1)
                        elif step == 2:
                            act.activation(vT_sb[s], bank[:, :], ACT.Identity, bias=b2_col[:, 0:1])\
                               .then_inc(s_l0_ev[s], 1)
                        else:
                            act.copy(v_hi[s][:, :, :], bank[:, :].rearrange("p (t c) -> p t c", t=T))\
                               .then_inc(s_l0_hi[s], 1)

            def layernorm(j):
                act.wait_ge(s_ln[j], LN_CENTERED)
                act.activation(G[:, :], X[:, :, :].rearrange("p t c -> p (t c)"), ACT.Square).then_inc(s_ln[j], 1)
                act.wait_ge(s_ln[j], LN_VAR)
                act.activation(root[:, :], vare[:, :], ACT.Sqrt).then_inc(s_ln[j], 1)

            def high_half_x(j):
                act.wait_ge(s_ln[2 * j], LN_STEPS)

                def body(i):
                    for s in range(4):
                        value_wait(act, s_xt_pe[j], 4 * i + s - 3)
                        act.copy(x_st[s][:, :, 0, :], X[:, :, bass.ds((4 * i + s) * D, D)]).then_inc(s_xt_hi[j], 1)
                body(0)
                with act.Fori(1, B // 4) as i:
                    body(i)

            def attention(ph):
                kd = ph.k

                def body(i):
                    for k in range(8):
                        u, t = k // T, k % T
                        q, n = 2 * i + u, 8 * i + k
                        other = (u + 1) % 2
                        if t == 3 and ph.kind == "heads" and exists(q - 2, ph.units):
                            value_wait(act, ph.AV, q - 1)
                            value_wait(act, ph.z, q - 2)
                            act.activation(rel[:, :], banks[6 + u][:, :], ACT.Relu, scale=0.99).then_inc(ph.rel, 1)
                        if ph.kind == "last" and exists(n, ph.tiles):
                            value_wait(act, ph.es, q + 1)
                            value_wait(act, ph.lr, n - 1)
                            act.activation(t1[:, k % 2, :], banks[u][:, :], ACT.Identity,
                                           bias=es[:, u, t, 0:1]).then_inc(ph.t1, 1)
                        if t == 2 and exists(q + 1, ph.units):
                            value_wait(act, ph.h_pe, q + 2)
                            act.copy(hf[0:kd, other, :], banks[4][0:kd, :]).then_inc(ph.hf, 1)
                            if ph.kind != "last":
                                act.copy(hr[0:kd, other, :], banks[4][0:kd, :]).then_inc(ph.hr, 1)
                        if exists(n - LAG, ph.tiles):
                            kp = (k - LAG) % 8
                            value_wait(act, ph.T, n - LAG + 1)
                            value_wait(act, ph.AV, (q if t >= LAG else q - 1) - 1)
                            act.copy(pT[:, kp // T, :, (kp % T) * P:(kp % T + 1) * P],
                                     banks[2 + kp % 2][:, :].rearrange("p (m c) -> p m c", m=T)).then_inc(ph.PT, 1)
                        if ph.kind == "last":
                            if exists(n - 1, ph.tiles):
                                kp = (k - 1) % 8
                                value_wait(act, ph.neg, n)
                                value_wait(act, ph.T, n - 4)
                                value_wait(act, ph.rec, (q if t >= 1 else q - 1) - 1)
                                act.activation(pr[:, kp % 4, :], sc[:, kp % 4, :], ACT.Exp,
                                               bias=ng[:, kp % 4:kp % 4 + 1],
                                               accum_out=ls[:, kp // T, kp % T:kp % T + 1]).then_inc(ph.E, 1)
                        elif exists(n, ph.tiles):
                            value_wait(act, ph.neg, n + 1)
                            value_wait(act, ph.P, n - 3)
                            act.activation(ex[:, k % 4, :], sc[:, k % 4, :], ACT.Exp,
                                           bias=ng[:, k % 4:k % 4 + 1]).then_inc(ph.E, 1)
                iterations(act, ph.units, body)

            layernorm(0)
            high_half_x(0)
            attention(heads)
            attention(outer)
            act.wait_ge(s_deg, 1)
            act.activation(root[:, 0:T], deg[:, :], ACT.Sqrt).then_inc(s_deg, 1)
            for t in range(T):
                act.wait_ge(s_deg2, 2 + t)
                act.copy(AT_hi[:, t, :], AT[:, t, :]).then_inc(s_at2_hi, 1)
            layernorm(1)

            for i in range(B // 2 // SLOTS):
                for s in range(SLOTS):
                    act.wait_ge(s_l2_x[s], i + 1)
                    act.copy(v_hi[s][:, :, :], v_st[s][:, :, :]).then_inc(s_l2_hi[s], 1)
                for s in range(SLOTS):
                    act.wait_ge(s_l2_pe[s], 2 * i + 1)
                    act.copy(eT_sb[s], banks[2 * s][:, :]).then_inc(s_l2_ev[s], 1)
            layernorm(2)
            high_half_x(1)
            attention(last)
            layernorm(3)

        @block.tensor
        def _(pe):
            def transpose(to, of, parts=P):
                return pe.transpose(to, of, ident[0:parts, 0:parts])

            pe.wait_ge(s_id, 1)
            pe.wait_ge(s_adj, 16 * T)
            for mt in range(T):
                for t in range(T):
                    mm = transpose(banks[mt][:, t * P:(t + 1) * P], A[:, t, mt * P:(mt + 1) * P])
                mm.then_inc(s_at_pe, 1)
            pe.wait_ge(s_wts, 16 * N_WTS)
            for j in range(4):
                mm = transpose(banks[4][:, j * D:(j + 1) * D], w_dup[:, j, :, :].rearrange("p c k -> p (c k)"), D)
            mm.then_inc(s_wdup_pe, 1)
            pe.wait_ge(s_bd, 8)
            pe.wait_ge(s_at_hi, T)
            pe.wait_ge(s_at_lo, T)

            def split_product(bank, s):
                for m in range(T):
                    pe.matmul(bank[:, :], v_hi[s][:, m, :], AT_hi[:, m, :], start=(m == 0), stop=False)
                    pe.matmul(bank[:, :], v_hi[s][:, m, :], AT_lo[:, m, :], start=False, stop=False)
                    mm = pe.matmul(bank[:, :], v_lo[s][:, m, :], AT_hi[:, m, :], start=False, stop=(m == T - 1))
                return mm

            pe.wait_ge(s_iv, 16 * B)
            for i in range(B // 2 // SLOTS):
                for g in range(GROUPS0):
                    step = (g - 1) % 4
                    for s in range(SLOTS):
                        bank = banks[2 * s + g % 2]
                        value_wait(pe, s_l0_ev[s], GROUPS0 * i + g)
                        if g == 0:
                            for t in range(T):
                                c = (SLOTS * i + s) * 2 * D
                                mm = transpose(bank[:, t * P:(t + 1) * P], V[:, t, c:c + 2 * D])
                        elif step == 0:
                            if g == 1:
                                pe.wait_ge(s_l0_stage[s], i + 1)
                            mm = split_product(bank, s)
                        elif step == 1:
                            pe.matmul(bank[:, :], w_bd[:, 0, :], vT_sb[s], start=True, stop=False)
                            mm = pe.matmul(bank[:, :], w_bd[:, 1, :], eT_sb[s], start=False, stop=True)
                        elif step == 2:
                            mm = pe.matmul(bank[:, :], w_bd[:, 2, :], hT_sb[s], start=True, stop=True)
                        else:
                            for t in range(T):
                                mm = transpose(bank[:, t * P:(t + 1) * P], vT_sb[s][:, t * P:(t + 1) * P])
                        mm.then_inc(s_l0_pe[s], 1)
            for s in range(SLOTS):
                pe.wait_ge(s_l0_ev[s], GROUPS0 * (B // 2 // SLOTS))

            def transposed_x(j):
                def body(i):
                    for s in range(4):
                        value_wait(pe, s_xt_st[j], 4 * i + s + 1)
                        value_wait(pe, s_xt[j], 4 * i + s - 3)
                        pe.nop(nofuse=True)
                        for t in range(T):
                            mm = transpose(banks[s][:, t * P:(t + 1) * P],
                                           x_st[s][:, t, :, :].rearrange("p c d -> p (c d)").bitcast(F32))
                        mm.then_inc(s_xt_pe[j], 1)
                body(0)
                with pe.Fori(1, B // 4) as i:
                    body(i)
                pe.wait_ge(s_xt[j], B)

            def attention(ph):
                kd = ph.k

                def hidden(i, u, q, hi, lo):
                    xt = XT[:, bass.ds(batch_of(ph, i, u + 1) * N, N)]
                    pe.matmul(banks[4][:, :], hi, xt, start=True, stop=False)
                    pe.matmul(banks[4][:, :], lo, xt, start=False, stop=True).then_inc(ph.h_pe, 1)

                def body(i):
                    for k in range(8):
                        u, t = k // T, k % T
                        q, n = 2 * i + u, 8 * i + k
                        other = (u + 1) % 2
                        if ph.kind != "last" and exists(n, ph.tiles):
                            value_wait(pe, ph.hr, q + 1)
                            value_wait(pe, ph.hl, q + 1)
                            value_wait(pe, ph.mx, n - 1)
                            high, low = hr[0:kd, u, t * P:(t + 1) * P], hl[0:kd, u, t * P:(t + 1) * P]
                            pe.matmul(banks[k % 2][:, :], high, hr[0:kd, u, :], start=True, stop=False)
                            pe.matmul(banks[k % 2][:, :], high, hl[0:kd, u, :], start=False, stop=False)
                            pe.matmul(banks[k % 2][:, :], low, hr[0:kd, u, :], start=False, stop=True)\
                              .then_inc(ph.S, 1)
                        if exists(n - LAG, ph.tiles):
                            kp = (k - LAG) % 8
                            value_wait(pe, ph.E if ph.kind == "last" else ph.P, n - LAG + 1)
                            value_wait(pe, ph.PT, n - LAG - 1)
                            for m in range(T):
                                mm = transpose(banks[2 + kp % 2][:, m * P:(m + 1) * P],
                                               pr[:, kp % 4, m * P:(m + 1) * P])
                            mm.then_inc(ph.T, 1)
                        qa, slot, part = (q - 1, other, 0) if t == 3 else (q - 2, u, t + 1)
                        if exists(qa, ph.units):
                            if part == 0:
                                value_wait(pe, ph.PT, 4 * qa + 4)
                                value_wait(pe, ph.hb, qa + 1)
                                value_wait(pe, ph.z, qa - 1)
                            if ph.kind == "heads":
                                mm = pe.matmul(banks[6 + slot][:, :], hb[:, slot, part, :], pT[:, slot, part, :],
                                               start=(part == 0), stop=(part == T - 1))
                            else:
                                for m in range(T):
                                    mm = pe.matmul(banks[6 + slot][:, part * D:(part + 1) * D],
                                                   pT[:, slot, m, part * P:(part + 1) * P], hb[:, slot, m, 0:D],
                                                   start=(m == 0), stop=(m == T - 1))
                            if part == T - 1:
                                mm.then_inc(ph.AV, 1)
                        if t == 1 and exists(q + 1, ph.units):
                            if ph.kind == "heads":
                                value_wait(pe, ph.hb, q)
                                value_wait(pe, ph.wh, q + 2)
                                hidden(i, u, q, wh_hi[other][:, :], wh_lo[other][:, :])
                            elif ph.kind == "outer":
                                value_wait(pe, ph.hr, q + 1)
                                value_wait(pe, ph.stage, q + 2)
                                pe.nop(nofuse=True)
                                for m in range(T):
                                    mm = transpose(banks[4][0:D, m * P:(m + 1) * P], g_st[:, m, :])
                                mm.then_inc(ph.h_pe, 1)
                            else:
                                value_wait(pe, ph.hb, q)
                                hidden(i, u, q, W3_hi[:, :, :].rearrange("i c o -> i (c o)"),
                                       W3_lo[:, :, :].rearrange("i c o -> i (c o)"))
                        if t == 2 and ph.kind == "heads" and exists(q - 3, ph.units):
                            value_wait(pe, ph.z, q - 2)
                            value_wait(pe, ph.G, q - 3)
                            value_wait(pe, s_wo[other], 16 * (i - 1 + u))
                            for m in range(T):
                                mm = pe.matmul(banks[5][:, m * D:(m + 1) * D], z[:, m * P:(m + 1) * P],
                                               wo_slot[other][:, :], start=True, stop=True)
                            mm.then_inc(ph.G_pe, 1)
                        if t == 3 and ph.kind != "outer" and exists(q, ph.units):
                            value_wait(pe, ph.hr if ph.kind == "heads" else ph.hf,
                                       q + 2 if exists(q + 1, ph.units) else q + 1)
                            w = kd
                            if ph.kind == "last":
                                pe.nop(nofuse=True)
                            for m in range(T):
                                mm = transpose(banks[4][:, m * w:(m + 1) * w], hf[0:kd, u, m * P:(m + 1) * P], kd)
                            mm.then_inc(ph.hn_pe, 1)
                        if t == 3 and ph.kind == "last" and exists(q + 1, ph.units):
                            value_wait(pe, ph.hf, q + 2)
                            value_wait(pe, ph.es, q + 1)
                            value_wait(pe, ph.t1, 4 * q)
                            for m in range(T):
                                pe.matmul(banks[5][:, 2 * m:2 * m + 2], hf[0:D, other, m * P:(m + 1) * P],
                                          a_src[:, :], start=True, stop=True)
                            pe.matmul(banks[other][:, :], a_dst_bc[:, :], hf[0:D, other, :],
                                      start=True, stop=True).then_inc(ph.es_pe, 1)
                if ph.kind == "outer":
                    pe.wait_ge(heads.G, heads.units)
                if ph.kind == "last":
                    pe.wait_ge(s_adb, 1)
                    pe.wait_ge(s_w3, 2)
                iterations(pe, ph.units, body)

            transposed_x(0)
            attention(heads)
            attention(outer)

            pe.wait_ge(s_at2_hi, T)
            pe.wait_ge(s_at2_lo, T)
            pe.wait_ge(outer.z, outer.units)
            for i in range(B // 2 // SLOTS):
                for s in range(SLOTS):
                    pe.wait_ge(s_l2_stage[s], i + 1)
                    value_wait(pe, s_l2_ev[s], 2 * i)
                    split_product(banks[2 * s], s).then_inc(s_l2_pe[s], 1)
                for s in range(SLOTS):
                    pe.wait_ge(s_l2_ev[s], 2 * i + 1)
                    for t in range(T):
                        mm = pe.matmul(banks[2 * s + 1][:, t * P:(t + 1) * P], eT_sb[s][:, t * P:(t + 1) * P],
                                       w_bd[:, 3, :], start=True, stop=True)
                    mm.then_inc(s_l2_pe[s], 1)
            for s in range(SLOTS):
                pe.wait_ge(s_l2_ev[s], 2 * (B // 2 // SLOTS))
            transposed_x(1)
            attention(last)

        @block.vector
        def _(dve):
            dve.wait_ge(s_wdup_pe, 1)
            dve.wait_ge(s_bd0, 1)
            for j in range(4):
                for c in range(2):
                    dve.tensor_copy(w_bd[c * D:(c + 1) * D, j, c * D:(c + 1) * D],
                                    banks[4][c * D:(c + 1) * D, j * D:(j + 1) * D]).then_inc(s_bd, 1)
            dve.tensor_copy(a_dst_bc[:, :], a_dst[:, 0:1].to_broadcast([D, P])).then_inc(s_adb, 1)
            for mt in range(T):
                dve.wait_ge(s_at_hi, mt + 1)
                dve.tensor_tensor(AT_lo[:, mt, :], AT[:, mt, :], AT_hi[:, mt, :].bitcast(F32),
                                  ALU.subtract).then_inc(s_at_lo, 1)

            dve.wait_ge(s_x, 16 * T)
            for i in range(B // 2 // SLOTS):
                for g in range(GROUPS0):
                    step = (g - 1) % 4
                    for s in range(SLOTS):
                        value = g > 0 and step == 3
                        if s % 2 == 0 and not value:
                            continue
                        bank = banks[2 * s + g % 2]
                        if value and g < GROUPS0 - 1:
                            dve.wait_ge(s_l0_hi[s], (STEPS - 1) * i + (g - 1) // 4 + 1)
                        else:
                            dve.wait_ge(s_l0_pe[s], GROUPS0 * i + g + 1)
                        if g == 0:
                            ins = dve.tensor_copy(vT_sb[s], bank[:, :])
                        elif step == 0:
                            ins = dve.tensor_copy(eT_sb[s], bank[:, :])
                        elif step == 1:
                            ins = dve.tensor_scalar(hT_sb[s], bank[:, :], b1_col[:, 0:1], 0.0, ALU.add, ALU.max)
                        elif step == 2:
                            ins = dve.tensor_scalar(vT_sb[s], bank[:, :], b2_col[:, 0:1], None, ALU.add)
                        elif g < GROUPS0 - 1:
                            ins = dve.tensor_tensor(v_lo[s][:, :, :].rearrange("p t c -> p (t c)"), bank[:, :],
                                                    v_hi[s][:, :, :].rearrange("p t c -> p (t c)").bitcast(F32),
                                                    ALU.subtract)
                        else:
                            c = (SLOTS * i + s) * 2 * D
                            xs = X[:, :, c:c + 2 * D]
                            ins = dve.tensor_tensor(xs, bank[:, :].rearrange("p (t c) -> p t c", t=T), xs, ALU.add)
                        ins.then_inc(s_l0_ev[s], 1)

            def layernorm(j):
                sm = s_ln[j]
                count = [0]

                def step(ins):
                    count[0] += 1
                    ins.then_inc(sm, 1)
                    dve.wait_ge(sm, count[0])

                x3 = X[:, :, :].rearrange("p t (b d) -> p (t b) d", d=D)
                g3 = G[:, :].rearrange("p (g d) -> p g d", d=D)
                per_node = lambda a: a[:, :].unsqueeze(2).to_broadcast([P, GR, D])
                step(dve.tensor_reduce(mean[:, :], x3, AX.X, ALU.add))
                step(dve.tensor_scalar(mean[:, :], mean[:, :], -1.0 / D, None, ALU.mult))
                step(dve.tensor_tensor(x3, x3, per_node(mean), ALU.add))
                count[0] += 1
                dve.wait_ge(sm, count[0])
                step(dve.tensor_reduce(vare[:, :], g3, AX.X, ALU.add))
                step(dve.tensor_scalar(vare[:, :], vare[:, :], 1.0 / D, LN_EPS, ALU.mult, ALU.add))
                count[0] += 1
                dve.wait_ge(sm, count[0])
                step(dve.reciprocal(rstd[:, :], root[:, :]))
                step(dve.tensor_tensor(newt[:, :], rstd[:, :], rstd[:, :], ALU.mult))
                step(dve.tensor_tensor(newt[:, :], newt[:, :], vare[:, :], ALU.mult))
                step(dve.tensor_scalar(newt[:, :], newt[:, :], -0.5, 1.5, ALU.mult, ALU.add))
                step(dve.tensor_tensor(rstd[:, :], rstd[:, :], newt[:, :], ALU.mult))
                step(dve.tensor_tensor(x3, x3, per_node(rstd), ALU.mult))

            def attention(ph):
                done = ph.G if ph.kind == "heads" else ph.z

                def body(i):
                    for k in range(8):
                        u, t = k // T, k % T
                        q, n = 2 * i + u, 8 * i + k
                        other = (u + 1) % 2
                        if exists(n, ph.tiles):
                            if ph.kind == "last":
                                value_wait(dve, ph.t1, n + 1)
                                value_wait(dve, ph.mx, n - 1)
                                dve.scalar_tensor_tensor(out=lr[:, k % 2, :], in0=t1[:, k % 2, :], scalar=0.2,
                                                         in1=t1[:, k % 2, :], op0=ALU.mult, op1=ALU.max)\
                                   .then_inc(ph.lr, 1)
                                value_wait(dve, ph.lr, n + 1)
                                value_wait(dve, ph.E, n - 3)
                                src = lr[:, k % 2, :]
                            else:
                                value_wait(dve, ph.S, n + 1)
                                value_wait(dve, ph.P, n - 3)
                                src = banks[k % 2][:, :]
                            dve.nop(nofuse=True)
                            dve.tensor_tensor_reduce(sc[:, k % 4, :], src, A[:, t, :], 1.0, LOWEST, ALU.mult, ALU.max,
                                                     mx[:, k % 4:k % 4 + 1]).then_inc(ph.mx, 1)
                        if ph.kind != "last" and exists(n - 1, ph.tiles):
                            kp = (k - 1) % 8
                            value_wait(dve, ph.E, n)
                            value_wait(dve, ph.cc, n)
                            value_wait(dve, ph.T, n - 4)
                            value_wait(dve, ph.rec, (q if t >= 1 else q - 1) - 1)
                            dve.scalar_tensor_tensor(out=pr[:, kp % 4, :], in0=sc[:, kp % 4, :],
                                                     scalar=cc[:, kp % 4:kp % 4 + 1], in1=ex[:, kp % 4, :],
                                                     op0=ALU.not_equal, op1=ALU.mult,
                                                     accum_out=ls[:, kp // T, kp % T:kp % T + 1]).then_inc(ph.P, 1)
                        if t == 0 and exists(q - 1, ph.units):
                            value_wait(dve, ph.AV, q - 2)
                            if ph.kind != "outer":
                                value_wait(dve, ph.hn_pe, q)
                            if ph.kind == "heads":
                                value_wait(dve, s_bb[other], 16 * (i + u))
                                dve.tensor_tensor(hb[:, other, :, :],
                                                  banks[4][:, :].rearrange("p (t c) -> p t c", t=T),
                                                  bb_slot[other][:, :].unsqueeze(1).to_broadcast([P, T, HID]),
                                                  ALU.add).then_inc(ph.hb, 1)
                            elif ph.kind == "outer":
                                dve.tensor_copy(hb[:, other, :, 0:D],
                                                G[:, bass.ds(batch_of(ph, i, u - 1) * T * D, T * D)]
                                                .rearrange("p (t d) -> p t d", t=T)).then_inc(ph.hb, 1)
                            else:
                                dve.tensor_copy(hb[:, other, :, 0:D],
                                                banks[4][:, 0:T * D].rearrange("p (t c) -> p t c", t=T))\
                                   .then_inc(ph.hb, 1)
                        if t == 3 and ph.kind == "heads" and exists(q - 3, ph.units):
                            value_wait(dve, ph.G_pe, q - 2)
                            value_wait(dve, ph.G, q - 3)
                            value_wait(dve, ph.rec, q - 2)
                            for m in range(T):
                                gs = G[:, bass.ds(batch_of(ph, i, u - 3) * T * D + m * D, D)]
                                ins = dve.scalar_tensor_tensor(out=gs, in0=banks[5][:, m * D:(m + 1) * D],
                                                               scalar=rc[:, other, m:m + 1], in1=gs,
                                                               op0=ALU.mult, op1=ALU.add)
                            ins.then_inc(ph.G, 1)
                        if t == 3 and exists(q - 1, ph.units):
                            value_wait(dve, ph.E if ph.kind == "last" else ph.P, 4 * q)
                            value_wait(dve, done, q - 2)
                            dve.reciprocal(rc[:, other, :], ls[:, other, :]).then_inc(ph.rec, 1)
                        if t == 3 and exists(q - 2, ph.units):
                            if ph.kind == "heads":
                                value_wait(dve, ph.rel, q - 1)
                                value_wait(dve, ph.G_pe, q - 2)
                                dve.scalar_tensor_tensor(out=z[:, :], in0=banks[6 + u][:, :], scalar=0.01,
                                                         in1=rel[:, :], op0=ALU.mult, op1=ALU.add)\
                                   .then_inc(ph.z, 1)
                            else:
                                value_wait(dve, ph.AV, q - 1)
                                value_wait(dve, ph.rec, q - 1)
                                value_wait(dve, ph.z, q - 2)
                                bias = bo_bc if ph.kind == "outer" else bias3_bc
                                for m in range(T):
                                    ins = dve.scalar_tensor_tensor(out=y[:, m, :],
                                                                   in0=banks[6 + u][:, m * D:(m + 1) * D],
                                                                   scalar=rc[:, u, m:m + 1], in1=bias[:, :],
                                                                   op0=ALU.mult, op1=ALU.add)
                                ins.then_inc(ph.y, 1)
                                xs = X[:, :, bass.ds(batch_of(ph, i, u - 2) * D, D)]
                                res = y
                                if ph.kind == "outer":
                                    value_wait(dve, ph.y, 2 * q - 3)
                                    dve.scalar_tensor_tensor(out=y2[:, :, :], in0=y[:, :, :], scalar=0.01,
                                                             in1=y[:, :, :], op0=ALU.mult, op1=ALU.max)\
                                       .then_inc(ph.y, 1)
                                    value_wait(dve, ph.y, 2 * q - 2)
                                    res = y2
                                else:
                                    value_wait(dve, ph.y, q - 1)
                                dve.tensor_tensor(xs, xs, res[:, :, :], ALU.add).then_inc(ph.z, 1)
                        if t == 3 and ph.kind == "last" and exists(q + 1, ph.units):
                            value_wait(dve, ph.es_pe, q + 2)
                            dve.tensor_copy(es[:, other, :, :], banks[5][:, 0:2 * T].rearrange("p (t c) -> p t c", t=T))\
                               .then_inc(ph.es, 1)
                iterations(dve, ph.units, body)

            def transposed_x(j):
                def body(i):
                    for s in range(4):
                        value_wait(dve, s_xt_pe[j], 4 * i + s + 1)
                        dve.tensor_copy(XT[:, bass.ds((4 * i + s) * N, N)], banks[s][:, :]).then_inc(s_xt[j], 1)
                body(0)
                with dve.Fori(1, B // 4) as i:
                    body(i)

            for s in range(SLOTS):
                dve.wait_ge(s_l0_ev[s], GROUPS0 * (B // 2 // SLOTS))
            layernorm(0)
            transposed_x(0)
            dve.wait_ge(s_adj, 16 * T)
            dve.memset(G[:, :], 0.0).then_inc(s_gz, 1)
            dve.wait_ge(s_gz, 1)
            attention(heads)
            dve.wait_ge(heads.G, heads.units)
            attention(outer)
            dve.wait_ge(outer.z, outer.units)

            dve.tensor_reduce(deg[:, :], A[:, :, :], AX.X, ALU.add).then_inc(s_deg2, 1)
            dve.wait_ge(s_deg2, 1)
            dve.tensor_scalar(deg[:, :], deg[:, :], 1.0, None, ALU.add).then_inc(s_deg, 1)
            for t in range(T):
                blk = AT[:, t, t * P:(t + 1) * P]
                dve.tensor_tensor(blk, blk, ident[:, :], ALU.add).then_inc(s_deg2, 1)
            dve.wait_ge(s_deg, 2)

            def step2(ins, n):
                ins.then_inc(s_deg, 1)
                dve.wait_ge(s_deg, n)
            for t in range(T):
                dve.wait_ge(s_at2_hi, t + 1)
                dve.tensor_tensor(AT_lo[:, t, :], AT[:, t, :], AT_hi[:, t, :].bitcast(F32),
                                  ALU.subtract).then_inc(s_at2_lo, 1)
            step2(dve.reciprocal(dinv[:, :], root[:, 0:T]), 3)
            step2(dve.tensor_tensor(newt[:, 0:T], dinv[:, :], dinv[:, :], ALU.mult), 4)
            step2(dve.tensor_tensor(newt[:, 0:T], newt[:, 0:T], deg[:, :], ALU.mult), 5)
            step2(dve.tensor_scalar(newt[:, 0:T], newt[:, 0:T], -0.5, 1.5, ALU.mult, ALU.add), 6)
            step2(dve.tensor_tensor(dinv[:, :], dinv[:, :], newt[:, 0:T], ALU.mult), 7)
            layernorm(1)

            for i in range(B // 2 // SLOTS):
                for s in range(SLOTS):
                    c = (SLOTS * i + s) * 2 * D
                    value_wait(dve, s_l2_stage[s], i)
                    for t in range(T):
                        ins = dve.tensor_scalar(v_st[s][:, t, :], X[:, t, c:c + 2 * D],
                                                dinv[:, t:t + 1], None, ALU.mult)
                    ins.then_inc(s_l2_x[s], 1)
                for s in range(SLOTS):
                    c = (SLOTS * i + s) * 2 * D
                    dve.wait_ge(s_l2_pe[s], 2 * i + 2)
                    for t in range(T):
                        xs = X[:, t, c:c + 2 * D]
                        ins = dve.scalar_tensor_tensor(out=xs, in0=banks[2 * s + 1][:, t * P:(t + 1) * P],
                                                       scalar=dinv[:, t:t + 1], in1=xs, op0=ALU.mult, op1=ALU.add)
                    ins.then_inc(s_l2_ev[s], 1)
            for s in range(SLOTS):
                dve.wait_ge(s_l2_ev[s], 2 * (B // 2 // SLOTS))
            layernorm(2)
            transposed_x(1)
            dve.wait_ge(s_a1, T)
            attention(last)
            dve.wait_ge(last.z, last.units)
            layernorm(3)


_INS = ["x", "adj", "L0_gnn_intervention_value", "L0_gnn_W1", "L0_gnn_b1", "L0_gnn_W2", "L0_gnn_b2",
        "L1_gnn_Wh", "L1_gnn_bh", "L1_gnn_W_out", "L1_gnn_b_out", "L2_gnn_W",
        "L3_gnn_weight", "L3_gnn_a", "L3_gnn_bias"]
_OUTS = [((B, N, D), "float32")]


def kernel(**inputs):
    import numpy as _np
    import concourse.bacc as _bacc
    from concourse import mybir as _mybir
    from concourse.bass_utils import run_bass_kernel_spmd as _run

    nc = _bacc.Bacc("TRN2", target_bir_lowering=False, num_devices=1)
    arrays, args = {}, []
    for name in _INS:
        a = _np.ascontiguousarray(inputs[name])
        arrays[f"in_{name}_dram"] = a
        args.append(nc.dram_tensor(f"in_{name}_dram", a.shape, _mybir.dt.from_np(a.dtype), kind="ExternalInput").ap())
    for i, (shape, dtype) in enumerate(_OUTS):
        dt = _mybir.dt.from_np(_np.dtype(dtype))
        args.append(nc.dram_tensor(f"out_{i}_dram", shape, dt, kind="ExternalOutput").ap())
    gnn_stack_program(nc, *args)
    r = _run(nc, [arrays], core_ids=[0])
    return r.results[0]["out_0_dram"]
```

```python
from contextlib import ExitStack

import concourse.bass as bass
from concourse import mybir

ALU = mybir.AluOpType
ACT = mybir.ActivationFunctionType
AX = mybir.AxisListType
F32 = mybir.dt.float32
F32R = mybir.dt.float32r
I32 = mybir.dt.int32

P = 128
B = 16
N = 512
D = 64
T = N // P
HEADS = 8
HID = 128
LN_EPS = 1e-5
CHUNKS = 4
SLOTS = 4
LAG = 3
LOWEST = -3.0e38


def value_wait(engine, semaphore, value):
    if not (isinstance(value, int) and value <= 0):
        engine.wait_ge(semaphore, value)


def exists(index, total):
    return 0 <= index < total if isinstance(index, int) else True


def gnn_stack_program(nc, x, adj, iv, W1, b1, W2, b2, Wh, bh, Wo, bo, W_l2, W_l3, a_l3, bias_l3, out):
    with ExitStack() as ctx:
        def sb(name, shape, dt=F32):
            return ctx.enter_context(nc.sbuf_tensor(name, shape, dt))

        def sem(name):
            return ctx.enter_context(nc.semaphore(name))

        X = sb("X", [P, T, B * D])
        G = sb("G", [P, B * T * D])
        V = G[:, :].rearrange("p (t c) -> p t c", t=T)
        XT = sb("XT", [P, B * N], F32R)
        A = sb("A", [P, T, N])
        AT_hi = sb("AT_hi", [P, T, N], F32R)
        AT_lo = sb("AT_lo", [P, T, N], F32R)
        ident = sb("ident", [P, P])
        w_bd = sb("w_bd", [P, 4, P])
        b1_col = sb("b1_col", [P, 1])
        b2_col = sb("b2_col", [P, 1])
        wm_hi = [sb(f"wm_hi{s}", [P, 4, HID], F32R) for s in range(2)]
        wm_lo = [sb(f"wm_lo{s}", [P, 4, HID], F32R) for s in range(2)]
        bb_pair = sb("bb_pair", [P, 2, HID])
        wo_slot = [sb(f"wo_slot{s}", [P, D]) for s in range(2)]
        bo_bc = sb("bo_bc", [P, D])
        W3_sb = sb("W3_sb", [P, 2, D])
        W3_hi = sb("W3_hi", [P, 2, D], F32R)
        W3_lo = sb("W3_lo", [P, 2, D], F32R)
        a_src = sb("a_src", [D, 2])
        a_dst = sb("a_dst", [D, 1])
        a_dst_bc = sb("a_dst_bc", [D, P])
        bias3_bc = sb("bias3_bc", [P, D])
        v_st_all = sb("v_st_all", [P, SLOTS, T, 2 * D])
        v_st = [v_st_all[:, s, :, :] for s in range(SLOTS)]
        wm_raw = v_st_all[:, :, :, :].rearrange("p h k o -> p h (k o)")
        v_hi_all = sb("v_hi_all", [P, SLOTS, T, 2 * D], F32R)
        v_lo_all = sb("v_lo_all", [P, SLOTS, T, 2 * D], F32R)
        v_hi = [v_hi_all[:, s, :, :] for s in range(SLOTS)]
        v_lo = [v_lo_all[:, s, :, :] for s in range(SLOTS)]
        GR = T * B
        mean = sb("mean", [P, GR])
        vare = sb("vare", [P, GR])
        root = sb("root", [P, GR])
        rstd = sb("rstd", [P, GR])
        newt = sb("newt", [P, GR])
        deg = sb("deg", [P, T])
        dinv = sb("dinv", [P, T])
        x_st_all = sb("x_st_all", [P, 4, T, 2 * D], F32R)
        x_st = [x_st_all[:, s, :, :].rearrange("p t (c d) -> p t c d", c=2) for s in range(4)]
        hf = sb("hf", [P, 2, N])
        hr = sb("hr", [P, 2, N], F32R)
        hl = sb("hl", [P, 2, N], F32R)
        hb = sb("hb", [P, 2, T, D])
        hb_hi = x_st_all
        hb_lo = sb("hb_lo", [P, 4, T, HID], F32R)
        xs = sb("xs", [P, N], F32R)
        sc = sb("sc", [P, 4, N])
        ex = sb("ex", [P, 4, N])
        pr = sb("pr", [P, 4, N])
        pT = sb("pT", [P, 2, T, N])
        pT_hi = v_hi_all[:, :, :, :].rearrange("p s t c -> p (s t c)").rearrange("p (u m n) -> p u m n", u=2, m=T)
        pT_lo = v_lo_all[:, :, :, :].rearrange("p s t c -> p (s t c)").rearrange("p (u m n) -> p u m n", u=2, m=T)
        pT_flat = pT[:, :, :, :].rearrange("p u m n -> p (u m n)")
        pT_left = pT_flat[:, 0:T * N].rearrange("p (u m n) -> p u m n", u=2, m=T)
        hb_heads = pT_flat[:, T * N:2 * T * N].rearrange("p (s t c) -> p s t c", s=4, t=T)
        AT = pT[:, 0, :, :]
        w_dup = ex[0:D, 0, :].rearrange("p (j c k) -> p j c k", j=4, c=2)
        whT = sc[:, 0:2, :]
        t1, lr = ex[:, 0:2, :], ex[:, 2:4, :]
        es = sb("es", [P, 2, T, 2])
        vT_sb = [ex[:, s, :] for s in range(SLOTS)]
        eT_sb = [sc[:, s, :] for s in range(SLOTS)]
        hT_sb = [pr[:, s, :] for s in range(SLOTS)]
        rel = sb("rel", [P, N])
        share = sb("share", [P, T, D])
        z = sb("z", [P, N])
        g_st = z[:, :].rearrange("p (t c d) -> p t c d", t=T, c=2)
        mx = sb("mx", [P, 4])
        ng = sb("ng", [P, 4])
        cc = sb("cc", [P, 4])
        ls = sb("ls", [P, 2, T])
        rc = sb("rc", [P, 2, T])
        y = sb("y", [P, T, D])
        y2 = share

        banks = [ctx.enter_context(nc.psum_tensor(f"bank{i}", [P, N], F32)) for i in range(8)]

        s_adj = sem("s_adj")
        s_v = sem("s_v")
        s_iv = sem("s_iv")
        s_x = sem("s_x")
        s_w0 = sem("s_w0")
        s_wraw = sem("s_wraw")
        s_wts = sem("s_wts")
        s_bb = sem("s_bb")
        s_wo = [sem(f"s_wo{s}") for s in range(2)]
        s_out = sem("s_out")
        s_idp = sem("s_idp")
        s_id = sem("s_id")
        s_bd0 = sem("s_bd0")
        s_wdup_pe = sem("s_wdup_pe")
        s_bd = sem("s_bd")
        s_whT_pe = sem("s_whT_pe")
        s_whT = sem("s_whT")
        s_m_pe = sem("s_m_pe")
        s_m = sem("s_m")
        s_adb = sem("s_adb")
        s_w3 = sem("s_w3")
        s_at_pe = sem("s_at_pe")
        s_at = sem("s_at")
        s_at_hi = sem("s_at_hi")
        s_at_lo = sem("s_at_lo")
        s_at2 = sem("s_at2")
        s_at2_hi = sem("s_at2_hi")
        s_at2_lo = sem("s_at2_lo")
        s_a1 = sem("s_a1")
        s_degsum = sem("s_degsum")
        s_deg = sem("s_deg")
        s_gz = sem("s_gz")
        s_l0_sthi = [sem(f"s_l0_sthi{s}") for s in range(SLOTS)]
        s_l0_stage = [sem(f"s_l0_stage{s}") for s in range(SLOTS)]
        s_l0_pe = [sem(f"s_l0_pe{s}") for s in range(SLOTS)]
        s_l0_hi = [sem(f"s_l0_hi{s}") for s in range(SLOTS)]
        s_l0_ev = [sem(f"s_l0_ev{s}") for s in range(SLOTS)]
        s_l2_x = [sem(f"s_l2_x{s}") for s in range(SLOTS)]
        s_l2_hi = [sem(f"s_l2_hi{s}") for s in range(SLOTS)]
        s_l2_stage = [sem(f"s_l2_stage{s}") for s in range(SLOTS)]
        s_l2_pe = [sem(f"s_l2_pe{s}") for s in range(SLOTS)]
        s_l2_ev = [sem(f"s_l2_ev{s}") for s in range(SLOTS)]
        s_ln_step = sem("s_ln_step")
        s_centered = sem("s_centered")
        s_squared = sem("s_squared")
        s_var = sem("s_var")
        s_root = sem("s_root")
        s_normed = sem("s_normed")
        s_xt_hi = [sem(f"s_xt_hi{j}") for j in range(2)]
        s_xt_st = [sem(f"s_xt_st{j}") for j in range(2)]
        s_xt_pe = [sem(f"s_xt_pe{j}") for j in range(2)]
        s_xt = [sem(f"s_xt{j}") for j in range(2)]

        N_W0, N_WTS = 4 + 4, 9
        CB = B // CHUNKS
        STEPS = 3
        GROUPS0 = 1 + 4 * STEPS

        class AttentionPhase:

            def __init__(self, kind, units, k):
                self.kind, self.units, self.tiles, self.k = kind, units, units * T, k
                self.h_pe = sem(f"{kind}_h_pe")
                self.hf = sem(f"{kind}_hf")
                self.hb = sem(f"{kind}_hb")
                self.mx = sem(f"{kind}_mx")
                self.neg = sem(f"{kind}_neg")
                self.E = sem(f"{kind}_E")
                self.T = sem(f"{kind}_T")
                self.PT = sem(f"{kind}_PT")
                self.rec = sem(f"{kind}_rec")
                self.AV = sem(f"{kind}_AV")
                self.z = sem(f"{kind}_z")
                if kind == "outer":
                    self.hh = sem(f"{kind}_hh")
                    self.stage = sem(f"{kind}_stage")
                if kind != "last":
                    self.hr = sem(f"{kind}_hr")
                    self.hl = sem(f"{kind}_hl")
                    self.S = sem(f"{kind}_S")
                    self.cc = sem(f"{kind}_cc")
                    self.P = sem(f"{kind}_P")
                if kind != "outer":
                    self.hn_pe = sem(f"{kind}_hn_pe")
                if kind != "heads":
                    self.y = sem(f"{kind}_y")
                if kind == "heads":
                    self.xs = sem(f"{kind}_xs")
                    self.wm_hi = sem(f"{kind}_wm_hi")
                    self.wm = sem(f"{kind}_wm")
                    self.rel = sem(f"{kind}_rel")
                    self.hb_hi = sem(f"{kind}_hb_hi")
                    self.hb_lo = sem(f"{kind}_hb_lo")
                    self.PT_lo = sem(f"{kind}_PT_lo")
                    self.share = sem(f"{kind}_share")
                    self.G_pe = sem(f"{kind}_G_pe")
                    self.G = sem(f"{kind}_G")
                if kind == "last":
                    self.es_pe = sem(f"{kind}_es_pe")
                    self.es = sem(f"{kind}_es")
                    self.t1 = sem(f"{kind}_t1")
                    self.lr = sem(f"{kind}_lr")

        heads = AttentionPhase("heads", B * HEADS, HID)
        outer = AttentionPhase("outer", B, 2 * D)
        last = AttentionPhase("last", B, D)

        def iterations(engine, units, body):
            pairs = units // 2
            for i in (-1, 0, 1):
                body(i, i % 2)
            with engine.Fori(1, pairs // 2 - 1) as r:
                for p in (0, 1):
                    body(2 * r + p, p)
            for i in range(pairs - 2, pairs + 2):
                body(i, i % 2)

        def squares(c):
            return G[:, c * T * CB * D:(c + 1) * T * CB * D].rearrange("p (t c) -> p t c", t=T)

        def x_chunk(c):
            return X[:, :, c * CB * D:(c + 1) * CB * D]

        def wm_raw_pair(i):
            return wm_raw[:, :, :].rearrange("p h k -> p (h k)")[:, bass.ds(i // B * (4 * HID), 4 * HID)]

        def batch_of(ph, i, unit_in_pair):
            carry, u = divmod(unit_in_pair, 2)
            return (i + carry) % B if ph.kind == "heads" else 2 * (i + carry) + u

        block = ctx.enter_context(nc.Block())

        @block.sync
        def _(sp):
            for t in range(T):
                sp.dma_start(A[:, t, :], adj[t * P:(t + 1) * P, :]).then_inc(s_adj, 16)
            for t in range(T):
                sp.dma_start(V[:, t, :].rearrange("p (b d) -> p b d", b=B),
                             x[:, t * P:(t + 1) * P, :].rearrange("b p d -> p b d")).then_inc(s_v, 16)
            sp.wait_ge(s_v, 16 * T)
            sp.dma_start(V[0:1, 0, :].rearrange("a (b d) -> a b d", b=B),
                         iv.unsqueeze(1).to_broadcast([1, B, D])).then_inc(s_iv, 16)
            sp.dma_start(bo_bc[:, :], bo.partition_broadcast(P)).then_inc(s_wts, 16)
            sp.dma_start(bias3_bc[:, :], bias_l3.partition_broadcast(P)).then_inc(s_wts, 16)
            for c in range(2):
                for r in range(2):
                    sp.dma_start(W3_sb[r * D:(r + 1) * D, c, :], W_l3).then_inc(s_wts, 16)
                sp.dma_start(a_src[:, c:c + 1], a_l3[0:D, :]).then_inc(s_wts, 16)
            sp.dma_start(a_dst[:, :], a_l3[D:2 * D, :]).then_inc(s_wts, 16)
            for t in range(T):
                sp.dma_start(X[:, t, :].rearrange("p (b d) -> p b d", b=B),
                             x[:, t * P:(t + 1) * P, :].rearrange("b p d -> p b d")).then_inc(s_x, 16)

            pairs = B * HEADS // 2

            def load_biases(i):
                if exists(i, pairs):
                    value_wait(sp, heads.hb, 2 * i)
                    sp.dma_start(bb_pair[:, :, :], bh[bass.ds(i // B * 2, 2), :].rearrange("(a u) o -> a (u o)", a=1)
                                 .to_broadcast([P, 2 * HID])).then_inc(s_bb, 16)

            def load_projection(i, u):
                if exists(i, pairs):
                    value_wait(sp, heads.G_pe, 2 * i + u - 1)
                    sp.dma_start(wo_slot[u][:, :], Wo[bass.ds((i // B * 2 + u) * HID, HID), :])\
                      .then_inc(s_wo[u], 16)

            def head_weights(i):
                load_projection(i - 2, 0)
                load_biases(i)
                load_projection(i - 2, 1)

            for i in (0, 1, 2):
                head_weights(i)
            with sp.Fori(3, pairs) as i:
                head_weights(i)
            for i in (pairs, pairs + 1):
                head_weights(i)

            for c in range(CHUNKS):
                sp.wait_ge(s_normed, 3 * CHUNKS + c + 1)
                for t in range(T):
                    sp.dma_start(out[c * CB:(c + 1) * CB, t * P:(t + 1) * P, :].rearrange("b p d -> p b d"),
                                 x_chunk(c)[:, t, :].rearrange("p (b d) -> p b d", b=CB)).then_inc(s_out, 16)
            sp.wait_ge(s_out, 16 * T * CHUNKS)

        @block.gpsimd
        def _(pool):
            def after_wait():
                pool.nop(nofuse=True)

            nc.gpsimd.memset(ident[:, :], 0.0).then_inc(s_idp, 1)
            nc.gpsimd.memset(w_bd[:, :, :], 0.0).then_inc(s_bd0, 1)
            pool.wait_ge(s_idp, 1)
            nc.gpsimd.affine_select(out=ident[:, :], in_=ident[:, :], compare_op=ALU.not_equal, fill=1.0,
                                    base=0, pattern=[[-1, P]], channel_multiplier=1).then_inc(s_id, 1)
            pool.wait_ge(s_iv, 16)
            for i in range(B // 2 // SLOTS):
                for s in range(SLOTS):
                    vs = V[:, :, (SLOTS * i + s) * 2 * D:(SLOTS * i + s + 1) * 2 * D]
                    value_wait(pool, s_l0_pe[s], GROUPS0 * i - 3)
                    if i > 0:
                        pool.tensor_copy(v_hi[s][:, :, :], vs).then_inc(s_l0_sthi[s], 1)
                    pool.wait_ge(s_l0_sthi[s], i + 1)
                    pool.tensor_tensor(v_lo[s][:, :, :], vs, v_hi[s][:, :, :].bitcast(F32),
                                       ALU.subtract).then_inc(s_l0_stage[s], 1)

            pool.wait_ge(s_wts, 16 * N_WTS)
            pool.tensor_copy(W3_hi[:, :, :], W3_sb[:, :, :]).then_inc(s_w3, 1)
            pool.wait_ge(s_w3, 1)
            pool.tensor_tensor(W3_lo[:, :, :], W3_sb[:, :, :], W3_hi[:, :, :].bitcast(F32),
                               ALU.subtract).then_inc(s_w3, 1)

            def attention(ph):
                def body(i, p):
                    for k in range(8):
                        u, t = k // T, k % T
                        q, n = 2 * i + u, 8 * i + k
                        other = (u + 1) % 2
                        if exists(n, ph.tiles):
                            value_wait(pool, ph.mx, n + 1)
                            value_wait(pool, ph.E if ph.kind == "last" else ph.P, n - 3)
                            after_wait()
                            slot = slice(k % 4, k % 4 + 1)
                            pool.tensor_scalar(ng[:, slot], mx[:, slot], -1.0, None, ALU.mult).then_inc(ph.neg, 1)
                            if ph.kind != "last":
                                pool.tensor_scalar(cc[:, slot], mx[:, slot], 0.0, None, ALU.is_equal)\
                                    .then_inc(ph.cc, 1)
                        if t == 0 and ph.kind == "heads" and exists(q - 4, ph.units):
                            value_wait(pool, ph.share, q - 3)
                            after_wait()
                            gs = G[:, bass.ds(batch_of(ph, i, u - 4) * T * D, T * D)]
                            pool.tensor_tensor(gs, gs, share[:, :, :].rearrange("p t d -> p (t d)"), ALU.add)\
                                .then_inc(ph.G, 1)
                        if t == 1 and ph.kind == "heads" and exists(q, ph.units):
                            value_wait(pool, ph.hb_hi, q + 1)
                            after_wait()
                            pool.tensor_tensor(hb_lo[:, 2 * p:2 * p + 2, 2 * u:2 * u + 2, :],
                                               hb_heads[:, 2 * p:2 * p + 2, 2 * u:2 * u + 2, :],
                                               hb_hi[:, 2 * p:2 * p + 2, 2 * u:2 * u + 2, :].bitcast(F32),
                                               ALU.subtract).then_inc(ph.hb_lo, 1)
                        if t == (2 if ph.kind == "heads" else 1) and ph.kind != "last" and exists(q + 1, ph.units):
                            value_wait(pool, ph.hr, q + 2)
                            after_wait()
                            pool.tensor_tensor(hl[0:ph.k, other, :], hf[0:ph.k, other, :],
                                               hr[0:ph.k, other, :].bitcast(F32), ALU.subtract).then_inc(ph.hl, 1)
                        if t == 2 and ph.kind == "outer" and exists(q + 2, ph.units):
                            value_wait(pool, ph.h_pe, q + 2)
                            after_wait()
                            pool.tensor_copy(g_st[:, :, :, :], G[:, bass.ds(batch_of(ph, i, u + 2) * T * D, T * D)]
                                             .rearrange("p (t d) -> p t d", t=T).unsqueeze(2)
                                             .to_broadcast([P, T, 2, D])).then_inc(ph.stage, 1)
                        if t == 3 and u == 0 and ph.kind == "heads" and exists(i + 1, ph.units // 2):
                            value_wait(pool, ph.wm_hi, i + 2)
                            after_wait()
                            pool.tensor_tensor(wm_lo[1 - p][:, :, :].rearrange("p k o -> p (k o)"),
                                               wm_raw_pair(i + 1),
                                               wm_hi[1 - p][:, :, :].rearrange("p k o -> p (k o)").bitcast(F32),
                                               ALU.subtract).then_inc(ph.wm, 1)
                if ph.kind == "outer":
                    pool.wait_ge(heads.G, heads.units)
                iterations(pool, ph.units, body)

            def low_half_x(j):
                def body(i):
                    for s in range(4):
                        value_wait(pool, s_xt_hi[j], 4 * i + s + 1)
                        after_wait()
                        pool.tensor_tensor(x_st[s][:, :, 1, :], X[:, :, bass.ds((4 * i + s) * D, D)],
                                           x_st[s][:, :, 0, :].bitcast(F32), ALU.subtract).then_inc(s_xt_st[j], 1)
                body(0)
                if j == 0:
                    for s in range(SLOTS):
                        pool.wait_ge(s_l0_pe[s], GROUPS0 * (B // 2 // SLOTS) - 3)
                    for t in range(T):
                        blk = AT[:, t, t * P:(t + 1) * P]
                        pool.tensor_tensor(blk, blk, ident[:, :], ALU.add).then_inc(s_at2, 1)
                    for t in range(T):
                        pool.wait_ge(s_at2_hi, t + 1)
                        pool.tensor_tensor(AT_lo[:, t, :], AT[:, t, :], AT_hi[:, t, :].bitcast(F32),
                                           ALU.subtract).then_inc(s_at2_lo, 1)
                with pool.Fori(1, B // 4) as i:
                    body(i)

            low_half_x(0)
            attention(heads)
            attention(outer)

            for i in range(B // 2 // SLOTS):
                for s in range(SLOTS):
                    pool.wait_ge(s_l2_hi[s], i + 1)
                    pool.tensor_tensor(v_lo[s][:, :, :], v_st[s][:, :, :], v_hi[s][:, :, :].bitcast(F32),
                                       ALU.subtract).then_inc(s_l2_stage[s], 1)
            pool.wait_ge(s_deg, 1)
            for t in range(T):
                nc.gpsimd.affine_select(out=A[:, t, :], in_=A[:, t, :], compare_op=ALU.not_equal, fill=1.0,
                                        base=t * P, pattern=[[-1, N]], channel_multiplier=1).then_inc(s_a1, 1)
            low_half_x(1)
            attention(last)

        @block.scalar
        def _(act):
            for c in range(2):
                for u in range(2):
                    act.dma_start(wm_raw[c * D:(c + 1) * D, :, u * HID:(u + 1) * HID],
                                  Wh.rearrange("(h u) i o -> u i h o", u=2)[u]).then_inc(s_wraw, 16)

            for j, w in enumerate((W1[:, 0:D], W1[:, D:2 * D], W2, W_l2)):
                act.dma_start(w_dup[:, j, :, :], w.unsqueeze(1).to_broadcast([D, 2, D])).then_inc(s_w0, 16)
            for c in range(2):
                act.dma_start(b1_col[c * D:(c + 1) * D, :], b1.rearrange("(p a) -> p a", a=1)).then_inc(s_w0, 16)
                act.dma_start(b2_col[c * D:(c + 1) * D, :], b2.rearrange("(p a) -> p a", a=1)).then_inc(s_w0, 16)
            for mt in range(T):
                act.wait_ge(s_at_pe, mt + 1)
                nc.scalar.copy(AT[:, mt, :], banks[mt][:, :]).then_inc(s_at, 1)
                nc.scalar.copy(AT_hi[:, mt, :], banks[mt][:, :]).then_inc(s_at_hi, 1)
            for h in range(2):
                act.wait_ge(s_whT_pe, h + 1)
                nc.scalar.copy(whT[:, h, :], banks[5 + h][:, :]).then_inc(s_whT, 1)

            act.wait_ge(s_iv, 16)
            for s in range(SLOTS):
                act.copy(v_hi[s][:, :, :], V[:, :, s * 2 * D:(s + 1) * 2 * D]).then_inc(s_l0_sthi[s], 1)

            def square(j, c):
                act.wait_ge(s_centered, j * CHUNKS + c + 1)
                act.activation(squares(c), x_chunk(c), ACT.Square).then_inc(s_squared, 1)

            def take_root(j, c):
                act.wait_ge(s_var, j * CHUNKS + c + 1)
                act.activation(root[:, c * T * CB:(c + 1) * T * CB], vare[:, c * T * CB:(c + 1) * T * CB],
                               ACT.Sqrt).then_inc(s_root, 1)

            def evacuate_x(j, b):
                act.wait_ge(s_xt_pe[j], b + 1)
                act.copy(XT[:, b * N:(b + 1) * N], banks[b % 4][:, :]).then_inc(s_xt[j], 1)

            def high_half_x(j, c):
                act.wait_ge(s_normed, 2 * j * CHUNKS + c + 1)
                for b in range(c * CB, (c + 1) * CB):
                    if b >= 4:
                        evacuate_x(j, b - 4)
                    act.copy(x_st[b % 4][:, :, 0, :], X[:, :, b * D:(b + 1) * D]).then_inc(s_xt_hi[j], 1)

            for i in range(B // 2 // SLOTS):
                for g in range(GROUPS0 - 1):
                    step = (g - 1) % 4
                    for s in range(SLOTS):
                        value = g > 0 and step == 3
                        if s % 2 and not value:
                            continue
                        act.wait_ge(s_l0_pe[s], GROUPS0 * i + g + 1)
                        bank = banks[2 * s + g % 2]
                        if g == 0:
                            act.copy(vT_sb[s], bank[:, :]).then_inc(s_l0_ev[s], 1)
                        elif step == 0:
                            act.copy(eT_sb[s], bank[:, :]).then_inc(s_l0_ev[s], 1)
                        elif step == 1:
                            act.activation(hT_sb[s], bank[:, :], ACT.Relu, bias=b1_col[:, 0:1])\
                               .then_inc(s_l0_ev[s], 1)
                        elif step == 2:
                            act.activation(vT_sb[s], bank[:, :], ACT.Identity, bias=b2_col[:, 0:1])\
                               .then_inc(s_l0_ev[s], 1)
                        else:
                            act.copy(v_hi[s][:, :, :], bank[:, :].rearrange("p (t c) -> p t c", t=T))\
                               .then_inc(s_l0_hi[s], 1)
                    if i == 0 and g == 1:
                        act.wait_ge(s_deg, 1)
                        act.activation(root[:, 0:T], deg[:, :], ACT.Sqrt).then_inc(s_deg, 1)
                    if i == B // 2 // SLOTS - 1:
                        if g == 3:
                            for t in range(SLOTS):
                                act.wait_ge(s_l0_pe[t], GROUPS0 * i + 2)
                        if g in (3, 4):
                            square(0, g - 3)
                        if g in (5, 6):
                            take_root(0, g - 5)
                        if g == 9:
                            high_half_x(0, 0)
            for t in range(T):
                act.wait_ge(s_at2, t + 1)
                act.copy(AT_hi[:, t, :], AT[:, t, :]).then_inc(s_at2_hi, 1)

            def attention(ph):
                kd = ph.k

                def next_features(q, other):
                    value_wait(act, ph.h_pe, q + 2)
                    act.copy(hf[0:kd, other, :], banks[4][0:kd, :]).then_inc(ph.hf, 1)
                    if ph.kind != "last":
                        act.copy(hr[0:kd, other, :], banks[4][0:kd, :]).then_inc(ph.hr, 1)

                def body(i, p):
                    for k in range(8):
                        u, t = k // T, k % T
                        q, n = 2 * i + u, 8 * i + k
                        other = (u + 1) % 2
                        if t == 3 and ph.kind == "heads" and exists(q - 2, ph.units):
                            value_wait(act, ph.AV, q - 1)
                            value_wait(act, ph.z, q - 2)
                            act.activation(rel[:, :], banks[6 + u][:, :], ACT.Relu, scale=0.99).then_inc(ph.rel, 1)
                        if ph.kind == "last" and exists(n, ph.tiles):
                            value_wait(act, ph.es, q + 1)
                            value_wait(act, ph.lr, n - 1)
                            act.activation(t1[:, k % 2, :], banks[u][:, :], ACT.Identity,
                                           bias=es[:, u, t, 0:1]).then_inc(ph.t1, 1)
                        if t == 1 and ph.kind != "heads" and exists(q + 1, ph.units):
                            next_features(q, other)
                        if exists(n - LAG, ph.tiles):
                            kp = (k - LAG) % 8
                            value_wait(act, ph.T, n - LAG + 1)
                            value_wait(act, ph.AV, (q if t >= LAG else q - 1) - 1)
                            tiles = banks[2 + kp % 2][:, :].rearrange("p (m c) -> p m c", m=T)
                            if ph.kind == "heads" and kp % T >= 2:
                                act.copy(pT_hi[:, kp // T, :, (kp % T - 2) * P:(kp % T - 1) * P], tiles)\
                                   .then_inc(ph.PT, 1)
                            else:
                                whole = pT_left if ph.kind == "heads" else pT
                                act.copy(whole[:, kp // T, :, (kp % T) * P:(kp % T + 1) * P], tiles)\
                                   .then_inc(ph.PT, 1)
                        if t == 2 and ph.kind == "heads" and exists(q + 1, ph.units):
                            next_features(q, other)
                        if t == 1 and ph.kind == "heads" and exists(q, ph.units):
                            value_wait(act, ph.hb, q + 1)
                            act.copy(hb_hi[:, 2 * p:2 * p + 2, 2 * u:2 * u + 2, :],
                                     hb_heads[:, 2 * p:2 * p + 2, 2 * u:2 * u + 2, :]).then_inc(ph.hb_hi, 1)
                        if t == 0 and u == 1 and ph.kind == "heads" and exists(i + 1, ph.units // 2):
                            value_wait(act, ph.hn_pe, 2 * i + 2)
                            act.copy(xs[:, :], XT[:, bass.ds((i + 1) % B * N, N)]).then_inc(ph.xs, 1)
                        if t == 3 and u == 0 and ph.kind == "heads" and exists(i + 1, ph.units // 2):
                            value_wait(act, ph.hn_pe, 2 * i)
                            act.copy(wm_hi[1 - p][:, :, :].rearrange("p k o -> p (k o)"), wm_raw_pair(i + 1))\
                               .then_inc(ph.wm_hi, 1)
                        if ph.kind == "last":
                            if exists(n - 1, ph.tiles):
                                kp = (k - 1) % 8
                                value_wait(act, ph.neg, n)
                                value_wait(act, ph.T, n - 4)
                                value_wait(act, ph.rec, (q if t >= 1 else q - 1) - 1)
                                act.activation(pr[:, kp % 4, :], sc[:, kp % 4, :], ACT.Exp,
                                               bias=ng[:, kp % 4:kp % 4 + 1],
                                               accum_out=ls[:, kp // T, kp % T:kp % T + 1]).then_inc(ph.E, 1)
                        elif exists(n, ph.tiles):
                            value_wait(act, ph.neg, n + 1)
                            value_wait(act, ph.P, n - 3)
                            act.activation(ex[:, k % 4, :], sc[:, k % 4, :], ACT.Exp,
                                           bias=ng[:, k % 4:k % 4 + 1]).then_inc(ph.E, 1)
                        if t == 2 and ph.kind == "outer" and exists(q + 1, ph.units):
                            value_wait(act, ph.hl, q + 2)
                            act.copy(hl[0:D, other, :], hr[0:D, other, :]).then_inc(ph.hh, 1)
                iterations(act, ph.units, body)

            def layernorm(j):
                for k in range(CHUNKS + 2):
                    if k < CHUNKS:
                        square(j, k)
                    if 1 <= k <= CHUNKS:
                        take_root(j, k - 1)
                    if j == 1 and k in (2, 3):
                        for s in range((k - 2) * CB // 2, (k - 1) * CB // 2):
                            high_half_values(0, s)

            def high_half_values(i, s):
                act.wait_ge(s_l2_x[s], i + 1)
                act.copy(v_hi[s][:, :, :], v_st[s][:, :, :]).then_inc(s_l2_hi[s], 1)

            def evacuate_product(i, s):
                act.wait_ge(s_l2_pe[s], 2 * i + 1)
                act.copy(eT_sb[s], banks[2 * s][:, :]).then_inc(s_l2_ev[s], 1)

            square(0, 2)
            square(0, 3)
            high_half_x(0, 1)
            take_root(0, 2)
            take_root(0, 3)
            high_half_x(0, 2)
            high_half_x(0, 3)
            for b in range(B - 4, B):
                evacuate_x(0, b)
            attention(heads)
            attention(outer)
            layernorm(1)

            for i in range(B // 2 // SLOTS):
                for s in range(SLOTS):
                    evacuate_product(i, s)
                if i + 1 < B // 2 // SLOTS:
                    for s in range(SLOTS):
                        high_half_values(i + 1, s)
                if i > 0:
                    for c in range(2 * i - 2, 2 * i):
                        high_half_x(1, c)
                for c in range(2 * i, 2 * i + 2):
                    square(2, c)
                for c in range(2 * i, 2 * i + 2):
                    take_root(2, c)
            for c in range(CHUNKS - 2, CHUNKS):
                high_half_x(1, c)
            for b in range(B - 4, B):
                evacuate_x(1, b)
            attention(last)
            layernorm(3)

        @block.tensor
        def _(pe):
            def transpose(to, of, parts=P):
                return pe.transpose(to, of, ident[0:parts, 0:parts])

            pe.wait_ge(s_id, 1)
            pe.wait_ge(s_adj, 16 * T)
            for mt in range(T):
                for t in range(T):
                    mm = transpose(banks[mt][:, t * P:(t + 1) * P], A[:, t, mt * P:(mt + 1) * P])
                mm.then_inc(s_at_pe, 1)
            pe.wait_ge(s_wraw, 16 * 4)
            for h in range(HEADS):
                mm = transpose(banks[5 + h // 4][:, h % 4 * P:(h % 4 + 1) * P],
                               wm_raw[:, h // 2, h % 2 * HID:(h % 2 + 1) * HID])
                if h % 4 == 3:
                    mm.then_inc(s_whT_pe, 1)
            for h in range(HEADS):
                if h % 4 == 0:
                    pe.wait_ge(s_whT, h // 4 + 1)
                w = whT[:, h // 4, h % 4 * P:(h % 4 + 1) * P]
                mm = pe.matmul(banks[(7, 5)[h // 4]][:, h % 4 * P:(h % 4 + 1) * P], w, w, start=True, stop=True)
                if h % 4 == 3:
                    mm.then_inc(s_m_pe, 1)
            pe.wait_ge(s_w0, 16 * N_W0)
            for j in range(4):
                mm = transpose(banks[4][:, j * D:(j + 1) * D], w_dup[:, j, :, :].rearrange("p c k -> p (c k)"), D)
            mm.then_inc(s_wdup_pe, 1)
            pe.wait_ge(s_bd, 8)
            pe.wait_ge(s_m, 2)
            pe.wait_ge(s_at_hi, T)
            pe.wait_ge(s_at_lo, T)

            def split_product(bank, s):
                for m in range(T):
                    pe.matmul(bank[:, :], v_hi[s][:, m, :], AT_hi[:, m, :], start=(m == 0), stop=False)
                    pe.matmul(bank[:, :], v_hi[s][:, m, :], AT_lo[:, m, :], start=False, stop=False)
                    mm = pe.matmul(bank[:, :], v_lo[s][:, m, :], AT_hi[:, m, :], start=False, stop=(m == T - 1))
                return mm

            pe.wait_ge(s_iv, 16)
            for i in range(B // 2 // SLOTS):
                for g in range(GROUPS0):
                    step = (g - 1) % 4
                    for s in range(SLOTS):
                        bank = banks[2 * s + g % 2]
                        value_wait(pe, s_l0_ev[s], GROUPS0 * i + g)
                        if g == 0:
                            for t in range(T):
                                c = (SLOTS * i + s) * 2 * D
                                mm = transpose(bank[:, t * P:(t + 1) * P], V[:, t, c:c + 2 * D])
                        elif step == 0:
                            if g == 1:
                                pe.wait_ge(s_l0_stage[s], i + 1)
                            mm = split_product(bank, s)
                        elif step == 1:
                            pe.matmul(bank[:, :], w_bd[:, 0, :], vT_sb[s], start=True, stop=False)
                            mm = pe.matmul(bank[:, :], w_bd[:, 1, :], eT_sb[s], start=False, stop=True)
                        elif step == 2:
                            mm = pe.matmul(bank[:, :], w_bd[:, 2, :], hT_sb[s], start=True, stop=True)
                        else:
                            for t in range(T):
                                mm = transpose(bank[:, t * P:(t + 1) * P], vT_sb[s][:, t * P:(t + 1) * P])
                        mm.then_inc(s_l0_pe[s], 1)
            for s in range(SLOTS):
                pe.wait_ge(s_l0_ev[s], GROUPS0 * (B // 2 // SLOTS))

            def transposed_x(j):
                def body(i):
                    for s in range(4):
                        value_wait(pe, s_xt_st[j], 4 * i + s + 1)
                        value_wait(pe, s_xt[j], 4 * i + s - 3)
                        pe.nop(nofuse=True)
                        for t in range(T):
                            mm = transpose(banks[s][:, t * P:(t + 1) * P],
                                           x_st[s][:, t, :, :].rearrange("p c d -> p (c d)").bitcast(F32))
                        mm.then_inc(s_xt_pe[j], 1)
                body(0)
                with pe.Fori(1, B // 4) as i:
                    body(i)
                pe.wait_ge(s_xt[j], B)

            def attention(ph):
                kd = ph.k

                def hidden(i, u, hi, lo):
                    xt = XT[:, bass.ds(batch_of(ph, i, u + 1) * N, N)]
                    pe.matmul(banks[4][:, :], hi, xt, start=True, stop=False)
                    pe.matmul(banks[4][:, :], lo, xt, start=False, stop=True).then_inc(ph.h_pe, 1)

                def body(i, p):
                    for k in range(8):
                        u, t = k // T, k % T
                        q, n = 2 * i + u, 8 * i + k
                        other = (u + 1) % 2
                        if ph.kind != "last" and exists(n, ph.tiles):
                            value_wait(pe, ph.hr, q + 1)
                            value_wait(pe, ph.hl, q + 1)
                            value_wait(pe, ph.mx, n - 1)
                            tile = slice(t * P, (t + 1) * P)
                            if ph.kind == "heads":
                                xt = XT[:, bass.ds(batch_of(ph, i, u) * N, N)]
                                pe.matmul(banks[k % 2][:, :], hr[:, u, tile], xt, start=True, stop=False)
                                pe.matmul(banks[k % 2][:, :], hl[:, u, tile], xt, start=False, stop=True)\
                                  .then_inc(ph.S, 1)
                            else:
                                value_wait(pe, ph.hh, q + 1)
                                pe.matmul(banks[k % 2][:, :], hl[:, u, tile], hr[:, u, :], start=True, stop=False)
                                pe.matmul(banks[k % 2][:, :], hr[D:2 * D, u, tile], hl[D:2 * D, u, :],
                                          start=False, stop=True).then_inc(ph.S, 1)
                        if t == 2 and ph.kind == "last" and exists(q + 1, ph.units):
                            value_wait(pe, ph.hf, q + 2)
                            value_wait(pe, ph.es, q + 1)
                            value_wait(pe, ph.t1, 4 * q)
                            for m in range(T):
                                pe.matmul(banks[5][:, 2 * m:2 * m + 2], hf[0:D, other, m * P:(m + 1) * P],
                                          a_src[:, :], start=True, stop=True)
                            pe.matmul(banks[other][:, :], a_dst_bc[:, :], hf[0:D, other, :],
                                      start=True, stop=True).then_inc(ph.es_pe, 1)
                        if exists(n - LAG, ph.tiles):
                            kp = (k - LAG) % 8
                            value_wait(pe, ph.E if ph.kind == "last" else ph.P, n - LAG + 1)
                            value_wait(pe, ph.PT, n - LAG - 1)
                            if ph.kind == "heads" and kp % T < 2:
                                value_wait(pe, ph.PT_lo, 2 * (q if t == 3 else q - 1) + kp % T - 1)
                            for m in range(T):
                                mm = transpose(banks[2 + kp % 2][:, m * P:(m + 1) * P],
                                               pr[:, kp % 4, m * P:(m + 1) * P])
                            mm.then_inc(ph.T, 1)
                        if t == 3 and ph.kind == "heads" and exists(q + 1, ph.units):
                            w, first = (p, 2) if u == 0 else (1 - p, 0)
                            value_wait(pe, ph.hr, q + 2)
                            value_wait(pe, ph.xs, i + 1 + u)
                            for m in range(2):
                                node = xs[:, (first + m) * P:(first + m + 1) * P]
                                to = banks[4][:, m * 2 * HID:(m + 1) * 2 * HID]
                                pe.matmul(to, node, wm_hi[w][:, 0:2, :].rearrange("p k o -> p (k o)"),
                                          start=True, stop=False)
                                mm = pe.matmul(to, node, wm_lo[w][:, 0:2, :].rearrange("p k o -> p (k o)"),
                                               start=False, stop=True)
                            mm.then_inc(ph.hn_pe, 1)
                        qa, slot, part = (q - 1, other, 0) if t == 3 else (q - 2, u, t + 1)
                        if exists(qa, ph.units):
                            if part == 0:
                                value_wait(pe, ph.PT, 4 * qa + 4)
                                value_wait(pe, ph.hb, 2 * (i + u) if ph.kind == "heads" else qa + 1)
                                value_wait(pe, ph.z, qa - 1)
                            if ph.kind == "heads":
                                if part == 0:
                                    value_wait(pe, ph.PT_lo, 2 * qa + 2)
                                    value_wait(pe, ph.hb_hi, 2 * (i + u))
                                    value_wait(pe, ph.hb_lo, 2 * (i + u))
                                left, right = banks[6 + slot][:, 0:N // 2], banks[6 + slot][:, N // 2:N]
                                hs = 2 * p if (u, part) == (1, 0) else 2 * (1 - p) + slot
                                high, low = hb_hi[:, hs, part, :], hb_lo[:, hs, part, :]
                                pe.matmul(left, hb_heads[:, hs, part, :], pT_left[:, slot, part, :],
                                          start=(part == 0), stop=False)
                                pe.matmul(right, high, pT_hi[:, slot, part, :], start=False, stop=False)
                                pe.matmul(right, high, pT_lo[:, slot, part, :], start=False, stop=False)
                                mm = pe.matmul(right, low, pT_hi[:, slot, part, :], start=False,
                                               stop=(part == T - 1))
                            else:
                                for m in range(T):
                                    mm = pe.matmul(banks[6 + slot][:, part * D:(part + 1) * D],
                                                   pT[:, slot, m, part * P:(part + 1) * P], hb[:, slot, m, 0:D],
                                                   start=(m == 0), stop=(m == T - 1))
                            if part == T - 1:
                                mm.then_inc(ph.AV, 1)
                        if t == (1 if ph.kind == "heads" else 0) and exists(q + 1, ph.units):
                            if ph.kind == "heads":
                                value_wait(pe, ph.hb, q + 1)
                                value_wait(pe, ph.wm, i + 1 + u)
                                w = p if u == 0 else 1 - p
                                hidden(i, u, wm_hi[w][:, 2 + other, :], wm_lo[w][:, 2 + other, :])
                            elif ph.kind == "outer":
                                value_wait(pe, ph.hr, q + 1)
                                value_wait(pe, ph.stage, q + 2)
                                pe.nop(nofuse=True)
                                for m in range(T):
                                    mm = transpose(banks[4][:, m * P:(m + 1) * P],
                                                   g_st[:, m, :, :].rearrange("p c d -> p (c d)"))
                                mm.then_inc(ph.h_pe, 1)
                            else:
                                value_wait(pe, ph.hb, q)
                                hidden(i, u, W3_hi[:, :, :].rearrange("i c o -> i (c o)"),
                                       W3_lo[:, :, :].rearrange("i c o -> i (c o)"))
                        if t == 2 and ph.kind == "heads" and exists(q - 3, ph.units):
                            value_wait(pe, ph.z, q - 2)
                            value_wait(pe, ph.share, q - 3)
                            value_wait(pe, s_wo[other], 16 * (i - 1 + u))
                            for m in range(T):
                                mm = pe.matmul(banks[5][:, m * D:(m + 1) * D], z[:, m * P:(m + 1) * P],
                                               wo_slot[other][:, :], start=True, stop=True)
                            mm.then_inc(ph.G_pe, 1)
                        if t == 2 and ph.kind == "last" and exists(q, ph.units):
                            value_wait(pe, ph.hf, q + 2 if exists(q + 1, ph.units) else q + 1)
                            value_wait(pe, ph.hb, q)
                            w = kd
                            pe.nop(nofuse=True)
                            for m in range(T):
                                mm = transpose(banks[4][:, m * w:(m + 1) * w], hf[0:kd, u, m * P:(m + 1) * P], kd)
                            mm.then_inc(ph.hn_pe, 1)
                if ph.kind == "outer":
                    pe.wait_ge(heads.G, heads.units)
                if ph.kind == "last":
                    pe.wait_ge(s_adb, 1)
                    pe.wait_ge(s_w3, 2)
                iterations(pe, ph.units, body)

            transposed_x(0)
            attention(heads)
            attention(outer)

            pe.wait_ge(s_at2_hi, T)
            pe.wait_ge(s_at2_lo, T)
            pe.wait_ge(outer.z, outer.units)
            for i in range(B // 2 // SLOTS):
                for s in range(SLOTS):
                    pe.wait_ge(s_l2_stage[s], i + 1)
                    value_wait(pe, s_l2_ev[s], 2 * i)
                    split_product(banks[2 * s], s).then_inc(s_l2_pe[s], 1)
                for s in range(SLOTS):
                    pe.wait_ge(s_l2_ev[s], 2 * i + 1)
                    for t in range(T):
                        mm = pe.matmul(banks[2 * s + 1][:, t * P:(t + 1) * P], eT_sb[s][:, t * P:(t + 1) * P],
                                       w_bd[:, 3, :], start=True, stop=True)
                    mm.then_inc(s_l2_pe[s], 1)
            for s in range(SLOTS):
                pe.wait_ge(s_l2_ev[s], 2 * (B // 2 // SLOTS))
            transposed_x(1)
            attention(last)

        @block.vector
        def _(dve):
            dve.wait_ge(s_adj, 16 * T)
            dve.tensor_reduce(deg[:, :], A[:, :, :], AX.X, ALU.add).then_inc(s_degsum, 1)
            dve.wait_ge(s_degsum, 1)
            dve.tensor_scalar(deg[:, :], deg[:, :], 1.0, None, ALU.add).then_inc(s_deg, 1)
            for mt in range(T):
                dve.wait_ge(s_at_hi, mt + 1)
                dve.tensor_tensor(AT_lo[:, mt, :], AT[:, mt, :], AT_hi[:, mt, :].bitcast(F32),
                                  ALU.subtract).then_inc(s_at_lo, 1)

            dve.wait_ge(s_wdup_pe, 1)
            dve.wait_ge(s_bd0, 1)
            for j in range(4):
                for c in range(2):
                    dve.tensor_copy(w_bd[c * D:(c + 1) * D, j, c * D:(c + 1) * D],
                                    banks[4][c * D:(c + 1) * D, j * D:(j + 1) * D]).then_inc(s_bd, 1)
            for h in range(2):
                dve.wait_ge(s_m_pe, h + 1)
                dve.tensor_copy(wm_raw[:, 2 * h:2 * h + 2, 2 * HID:4 * HID],
                                banks[(7, 5)[h]][:, :].rearrange("p (a k) -> p a k", a=2)).then_inc(s_m, 1)
            steps = [0]

            def chained(ins):
                steps[0] += 1
                ins.then_inc(s_ln_step, 1)
                dve.wait_ge(s_ln_step, steps[0])

            def per_node(a):
                return a.rearrange("p (t b) -> p t b", t=T).unsqueeze(3).to_broadcast([P, T, CB, D])

            def stats(a, c):
                return a[:, c * T * CB:(c + 1) * T * CB]

            def center(j, c):
                x4 = x_chunk(c).rearrange("p t (b d) -> p t b d", d=D)
                m = stats(mean, c)
                chained(dve.tensor_reduce(m.rearrange("p (t b) -> p t b", t=T), x4, AX.X, ALU.add))
                chained(dve.tensor_scalar(m, m, -1.0 / D, None, ALU.mult))
                dve.tensor_tensor(x4, x4, per_node(m), ALU.add).then_inc(s_centered, 1)

            def variance(j, c):
                dve.wait_ge(s_squared, j * CHUNKS + c + 1)
                v = stats(vare, c)
                chained(dve.tensor_reduce(v.rearrange("p (t b) -> p t b", t=T),
                                       squares(c).rearrange("p t (b d) -> p t b d", d=D), AX.X, ALU.add))
                dve.tensor_scalar(v, v, 1.0 / D, LN_EPS, ALU.mult, ALU.add).then_inc(s_var, 1)

            def normalise(j, c):
                x4 = x_chunk(c).rearrange("p t (b d) -> p t b d", d=D)
                r, w = stats(rstd, c), stats(newt, c)
                dve.wait_ge(s_root, j * CHUNKS + c + 1)
                chained(dve.reciprocal(r, stats(root, c)))
                chained(dve.tensor_tensor(w, r, r, ALU.mult))
                chained(dve.tensor_tensor(w, w, stats(vare, c), ALU.mult))
                chained(dve.tensor_scalar(w, w, -0.5, 1.5, ALU.mult, ALU.add))
                chained(dve.tensor_tensor(r, r, w, ALU.mult))
                dve.tensor_tensor(x4, x4, per_node(r), ALU.mult).then_inc(s_normed, 1)

            def scale_values(i, s):
                c = (SLOTS * i + s) * 2 * D
                value_wait(dve, s_l2_stage[s], i)
                for t in range(T):
                    ins = dve.tensor_scalar(v_st[s][:, t, :], X[:, t, c:c + 2 * D],
                                            dinv[:, t:t + 1], None, ALU.mult)
                ins.then_inc(s_l2_x[s], 1)

            def layernorm(j):
                for k in range(CHUNKS + 2):
                    if k < CHUNKS:
                        center(j, k)
                    if 1 <= k <= CHUNKS:
                        variance(j, k - 1)
                    if k >= 2:
                        normalise(j, k - 2)
                        if j == 1:
                            dve.wait_ge(s_normed, j * CHUNKS + k - 1)
                            for p in range(CB // 2):
                                pair = (k - 2) * (CB // 2) + p
                                scale_values(pair // SLOTS, pair % SLOTS)

            for i in range(B // 2 // SLOTS):
                for g in range(GROUPS0):
                    step = (g - 1) % 4
                    for s in range(SLOTS):
                        value = g > 0 and step == 3
                        if s % 2 == 0 and not value:
                            continue
                        bank = banks[2 * s + g % 2]
                        if value and g < GROUPS0 - 1:
                            dve.wait_ge(s_l0_hi[s], (STEPS - 1) * i + (g - 1) // 4 + 1)
                        else:
                            dve.wait_ge(s_l0_pe[s], GROUPS0 * i + g + 1)
                        if g == 0:
                            ins = dve.tensor_copy(vT_sb[s], bank[:, :])
                        elif step == 0:
                            ins = dve.tensor_copy(eT_sb[s], bank[:, :])
                        elif step == 1:
                            ins = dve.tensor_scalar(hT_sb[s], bank[:, :], b1_col[:, 0:1], 0.0, ALU.add, ALU.max)
                        elif step == 2:
                            ins = dve.tensor_scalar(vT_sb[s], bank[:, :], b2_col[:, 0:1], None, ALU.add)
                        elif g < GROUPS0 - 1:
                            ins = dve.tensor_tensor(v_lo[s][:, :, :].rearrange("p t c -> p (t c)"), bank[:, :],
                                                    v_hi[s][:, :, :].rearrange("p t c -> p (t c)").bitcast(F32),
                                                    ALU.subtract)
                        else:
                            c = (SLOTS * i + s) * 2 * D
                            xs = X[:, :, c:c + 2 * D]
                            if (i, s) == (0, 0):
                                dve.wait_ge(s_x, 16 * T)
                            ins = dve.tensor_tensor(xs, bank[:, :].rearrange("p (t c) -> p t c", t=T), xs, ALU.add)
                        ins.then_inc(s_l0_ev[s], 1)
                    if i == 0 and g == 1:
                        dve.wait_ge(s_wts, 16 * N_WTS)
                        dve.tensor_copy(a_dst_bc[:, :], a_dst[:, 0:1].to_broadcast([D, P])).then_inc(s_adb, 1)
                    if i == 0 and g == 2:
                        dve.wait_ge(s_deg, 2)
                        chained(dve.reciprocal(dinv[:, :], root[:, 0:T]))
                        chained(dve.tensor_tensor(newt[:, 0:T], dinv[:, :], dinv[:, :], ALU.mult))
                        chained(dve.tensor_tensor(newt[:, 0:T], newt[:, 0:T], deg[:, :], ALU.mult))
                        chained(dve.tensor_scalar(newt[:, 0:T], newt[:, 0:T], -0.5, 1.5, ALU.mult, ALU.add))
                        chained(dve.tensor_tensor(dinv[:, :], dinv[:, :], newt[:, 0:T], ALU.mult))
                    if i == B // 2 // SLOTS - 1:
                        if g in (2, 3):
                            for pair in range((g - 2) * CB // 2, (g - 1) * CB // 2):
                                dve.wait_ge(s_l0_ev[pair], GROUPS0 * i)
                            center(0, g - 2)
                        if g in (4, 5):
                            variance(0, g - 4)
                        if g in (6, 7):
                            normalise(0, g - 6)

            def attention(ph):
                done = ph.share if ph.kind == "heads" else ph.z

                def body(i, p):
                    for k in range(8):
                        u, t = k // T, k % T
                        q, n = 2 * i + u, 8 * i + k
                        other = (u + 1) % 2
                        if exists(n, ph.tiles):
                            if ph.kind == "last":
                                value_wait(dve, ph.t1, n + 1)
                                value_wait(dve, ph.mx, n - 1)
                                dve.scalar_tensor_tensor(out=lr[:, k % 2, :], in0=t1[:, k % 2, :], scalar=0.2,
                                                         in1=t1[:, k % 2, :], op0=ALU.mult, op1=ALU.max)\
                                   .then_inc(ph.lr, 1)
                                value_wait(dve, ph.lr, n + 1)
                                value_wait(dve, ph.E, n - 3)
                                src = lr[:, k % 2, :]
                            else:
                                value_wait(dve, ph.S, n + 1)
                                value_wait(dve, ph.P, n - 3)
                                src = banks[k % 2][:, :]
                            dve.nop(nofuse=True)
                            dve.tensor_tensor_reduce(sc[:, k % 4, :], src, A[:, t, :], 1.0, LOWEST, ALU.mult, ALU.max,
                                                     mx[:, k % 4:k % 4 + 1]).then_inc(ph.mx, 1)
                        if t == 2 and ph.kind == "last" and exists(q + 1, ph.units):
                            value_wait(dve, ph.es_pe, q + 2)
                            dve.tensor_copy(es[:, other, :, :], banks[5][:, 0:2 * T].rearrange("p (t c) -> p t c", t=T))\
                               .then_inc(ph.es, 1)
                        if t == 0 and ph.kind == "heads" and exists(q, ph.units):
                            value_wait(dve, ph.hn_pe, q + 1)
                            value_wait(dve, ph.AV, 2 * i - 2)
                            value_wait(dve, s_bb, 16 * (i + 1))
                            dve.tensor_tensor(hb_heads[:, 2 * p:2 * p + 2, 2 * u:2 * u + 2, :],
                                              banks[4][:, :].rearrange("p (t h c) -> p h t c", t=2, h=2),
                                              bb_pair[:, :, :].unsqueeze(2).to_broadcast([P, 2, 2, HID]),
                                              ALU.add).then_inc(ph.hb, 1)
                        if ph.kind != "last" and exists(n - 1, ph.tiles):
                            kp = (k - 1) % 8
                            value_wait(dve, ph.E, n)
                            value_wait(dve, ph.cc, n)
                            value_wait(dve, ph.T, n - 4)
                            value_wait(dve, ph.rec, (q if t >= 1 else q - 1) - 1)
                            dve.scalar_tensor_tensor(out=pr[:, kp % 4, :], in0=sc[:, kp % 4, :],
                                                     scalar=cc[:, kp % 4:kp % 4 + 1], in1=ex[:, kp % 4, :],
                                                     op0=ALU.not_equal, op1=ALU.mult,
                                                     accum_out=ls[:, kp // T, kp % T:kp % T + 1]).then_inc(ph.P, 1)
                        if t in (1, 2) and ph.kind == "heads" and exists(q - 1, ph.units):
                            kp = (k - LAG) % 8
                            value_wait(dve, ph.PT, n - LAG + 1)
                            cols = slice((kp % T - 2) * P, (kp % T - 1) * P)
                            dve.tensor_tensor(pT_lo[:, other, :, cols],
                                              banks[2 + kp % 2][:, :].rearrange("p (m c) -> p m c", m=T),
                                              pT_hi[:, other, :, cols].bitcast(F32), ALU.subtract)\
                               .then_inc(ph.PT_lo, 1)
                        if t == 0 and ph.kind == "outer" and exists(q - 1, ph.units):
                            value_wait(dve, ph.AV, q - 2)
                            dve.tensor_copy(hb[:, other, :, 0:D],
                                            G[:, bass.ds(batch_of(ph, i, u - 1) * T * D, T * D)]
                                            .rearrange("p (t d) -> p t d", t=T)).then_inc(ph.hb, 1)
                        if t == 3 and ph.kind == "last" and exists(q, ph.units):
                            value_wait(dve, ph.AV, q - 1)
                            value_wait(dve, ph.hn_pe, q + 1)
                            dve.tensor_copy(hb[:, u, :, 0:D],
                                            banks[4][:, 0:T * D].rearrange("p (t c) -> p t c", t=T)).then_inc(ph.hb, 1)
                        if t == 3 and ph.kind == "heads" and exists(q - 3, ph.units):
                            value_wait(dve, ph.G_pe, q - 2)
                            value_wait(dve, ph.G, q - 3)
                            value_wait(dve, ph.rec, q - 2)
                            dve.tensor_tensor(share[:, :, :], banks[5][:, 0:T * D].rearrange("p (t d) -> p t d", t=T),
                                              rc[:, other, :].unsqueeze(2).to_broadcast([P, T, D]), ALU.mult)\
                               .then_inc(ph.share, 1)
                        if t == 3 and exists(q - 1, ph.units):
                            value_wait(dve, ph.E if ph.kind == "last" else ph.P, 4 * q)
                            value_wait(dve, done, q - 2)
                            dve.reciprocal(rc[:, other, :], ls[:, other, :]).then_inc(ph.rec, 1)
                        if t == 3 and exists(q - 2, ph.units):
                            if ph.kind == "heads":
                                value_wait(dve, ph.rel, q - 1)
                                value_wait(dve, ph.G_pe, q - 2)
                                dve.scalar_tensor_tensor(out=z[:, :], in0=banks[6 + u][:, :], scalar=0.01,
                                                         in1=rel[:, :], op0=ALU.mult, op1=ALU.add)\
                                   .then_inc(ph.z, 1)
                            else:
                                value_wait(dve, ph.AV, q - 1)
                                value_wait(dve, ph.rec, q - 1)
                                value_wait(dve, ph.z, q - 2)
                                bias = bo_bc if ph.kind == "outer" else bias3_bc
                                for m in range(T):
                                    ins = dve.scalar_tensor_tensor(out=y[:, m, :],
                                                                   in0=banks[6 + u][:, m * D:(m + 1) * D],
                                                                   scalar=rc[:, u, m:m + 1], in1=bias[:, :],
                                                                   op0=ALU.mult, op1=ALU.add)
                                ins.then_inc(ph.y, 1)
                                xs = X[:, :, bass.ds(batch_of(ph, i, u - 2) * D, D)]
                                res = y
                                if ph.kind == "outer":
                                    value_wait(dve, ph.y, 2 * q - 3)
                                    dve.scalar_tensor_tensor(out=y2[:, :, :], in0=y[:, :, :], scalar=0.01,
                                                             in1=y[:, :, :], op0=ALU.mult, op1=ALU.max)\
                                       .then_inc(ph.y, 1)
                                    value_wait(dve, ph.y, 2 * q - 2)
                                    res = y2
                                else:
                                    value_wait(dve, ph.y, q - 1)
                                dve.tensor_tensor(xs, xs, res[:, :, :], ALU.add).then_inc(ph.z, 1)
                iterations(dve, ph.units, body)

            for s in range(SLOTS):
                dve.wait_ge(s_l0_ev[s], GROUPS0 * (B // 2 // SLOTS))
            center(0, 2)
            center(0, 3)
            variance(0, 2)
            variance(0, 3)
            normalise(0, 2)
            normalise(0, 3)
            dve.memset(G[:, :], 0.0).then_inc(s_gz, 1)
            dve.wait_ge(s_gz, 1)
            attention(heads)
            dve.wait_ge(heads.G, heads.units)
            attention(outer)
            dve.wait_ge(outer.z, outer.units)

            layernorm(1)

            for i in range(B // 2 // SLOTS):
                for s in range(SLOTS):
                    c = (SLOTS * i + s) * 2 * D
                    dve.wait_ge(s_l2_pe[s], 2 * i + 2)
                    for t in range(T):
                        xs2 = X[:, t, c:c + 2 * D]
                        ins = dve.scalar_tensor_tensor(out=xs2, in0=banks[2 * s + 1][:, t * P:(t + 1) * P],
                                                       scalar=dinv[:, t:t + 1], in1=xs2, op0=ALU.mult, op1=ALU.add)
                    ins.then_inc(s_l2_ev[s], 1)
                for s in range(SLOTS):
                    dve.wait_ge(s_l2_ev[s], 2 * (i + 1))
                for c in range(2 * i, 2 * i + 2):
                    center(2, c)
                for c in range(2 * i, 2 * i + 2):
                    variance(2, c)
                for c in range(2 * i, 2 * i + 2):
                    normalise(2, c)
            dve.wait_ge(s_a1, T)
            attention(last)
            dve.wait_ge(last.z, last.units)
            layernorm(3)


_INS = ["x", "adj", "L0_gnn_intervention_value", "L0_gnn_W1", "L0_gnn_b1", "L0_gnn_W2", "L0_gnn_b2",
        "L1_gnn_Wh", "L1_gnn_bh", "L1_gnn_W_out", "L1_gnn_b_out", "L2_gnn_W",
        "L3_gnn_weight", "L3_gnn_a", "L3_gnn_bias"]
_OUTS = [((B, N, D), "float32")]


def kernel(**inputs):
    import numpy as _np
    import concourse.bacc as _bacc
    from concourse import mybir as _mybir
    from concourse.bass_utils import run_bass_kernel_spmd as _run

    nc = _bacc.Bacc("TRN2", target_bir_lowering=False, num_devices=1)
    arrays, args = {}, []
    for name in _INS:
        a = _np.ascontiguousarray(inputs[name])
        arrays[f"in_{name}_dram"] = a
        args.append(nc.dram_tensor(f"in_{name}_dram", a.shape, _mybir.dt.from_np(a.dtype), kind="ExternalInput").ap())
    for i, (shape, dtype) in enumerate(_OUTS):
        dt = _mybir.dt.from_np(_np.dtype(dtype))
        args.append(nc.dram_tensor(f"out_{i}_dram", shape, dt, kind="ExternalOutput").ap())
    gnn_stack_program(nc, *args)
    r = _run(nc, [arrays], core_ids=[0])
    return r.results[0]["out_0_dram"]
```
